# Optimizing a Trainium2 kernel written in Bass

```python
import numpy as np
import jax
import jax.numpy as jnp

def _softmax(x, axis=-1):
    return jax.nn.softmax(x, axis=axis)

def _gelu(x):
    return jax.nn.gelu(x, approximate=True)

def _silu(x):
    return jax.nn.silu(x)

def _sigmoid(x):
    return jax.nn.sigmoid(x)

def _layernorm(x, axis=-1, eps=1e-05):
    m = jnp.mean(x, axis=axis, keepdims=True)
    v = jnp.var(x, axis=axis, keepdims=True)
    return (x - m) / jnp.sqrt(v + eps)

def _scatter_add(tgt, idx, src, axis=0):
    return tgt.at[idx].add(src)

def _segment_sum(src, seg, n):
    return jax.ops.segment_sum(src, seg, n)
kernel_name = 'mk_decoder_preln_d1_seqx_r8_f12126'

def setup_inputs(seed: int=0):
    np.random.seed(seed)
    _w = jnp.asarray

    def _rec_inputs():
        import jax
        import jax.numpy as jnp
        _rk = jax.random.key(seed)
        x = 7.22e-05 + 1 * jax.random.normal(jax.random.fold_in(_rk, 1), (8, 128, 256), jnp.float32)
        _lenS = 128 - jax.random.randint(jax.random.fold_in(_rk, 7), (8,), 0, max(1, 128 // 4) + 1, jnp.int32)
        _lenS2 = 128 - jax.random.randint(jax.random.fold_in(_rk, 8), (8,), 0, max(1, 128 // 4) + 1, jnp.int32)
        _ctx_2048P = jax.random.normal(jax.random.fold_in(_rk, 11), (8, 16, 256), jnp.float32)
        _ctx_2048c = jax.random.dirichlet(jax.random.fold_in(_rk, 511), 0.3 * jnp.ones((16,), jnp.float32), (8, 128))
        _ctx_2048t = jnp.einsum('bsk,bkd->bsd', _ctx_2048c, _ctx_2048P)
        _ctx_2048t = _ctx_2048t * jax.lax.rsqrt(jnp.mean(jnp.square(_ctx_2048t)) + 1e-12) * 0.953939
        ctx_2048 = 4.13588e-05 + 0.999923 * (_ctx_2048t + 0.3 * jax.random.normal(jax.random.fold_in(_rk, 611), (8, 128, 256), jnp.float32))
        return (x, ctx_2048)
    x, ctx_2048 = _rec_inputs()

    def _L0_attn_setup():
        import jax, jax.numpy as jnp
        import numpy as np
        H, DK, DV = (16, 128, 128)
        EPS = 1e-06

        def _causal_dw_conv(x, w):
            K = w.shape[0]
            T = x.shape[1]
            xp = jnp.pad(x, ((0, 0), (K - 1, 0), (0, 0)))
            out = w[0] * xp[:, 0:T, :]
            for i in range(1, K):
                out = out + w[i] * xp[:, i:i + T, :]
            return out

        def _rmsnorm(h, w):
            hf = h.astype(jnp.float32)
            var = jnp.mean(hf * hf, axis=-1, keepdims=True)
            return (hf * jax.lax.rsqrt(var + EPS)).astype(h.dtype) * w

        def _l2norm(x):
            return x * jax.lax.rsqrt(jnp.sum(x * x, axis=-1, keepdims=True) + EPS)
        key = jax.random.key(seed)
        ks = jax.random.split(key, 32)
        B, T, D = (1, 128, 256)
        LOW, I = (128, 1024)
        KD, VD = (H * DK, H * DV)
        s = 0.02
        f = jnp.float32
        return {'x': jax.random.normal(ks[0], (B, T, D), f), 'wq': jax.random.normal(ks[1], (D, KD), f) * s, 'wk': jax.random.normal(ks[2], (D, KD), f) * s, 'wv': jax.random.normal(ks[3], (D, VD), f) * s, 'conv_q': jax.random.normal(ks[4], (4, KD), f) * 0.2, 'conv_k': jax.random.normal(ks[5], (4, KD), f) * 0.2, 'conv_v': jax.random.normal(ks[6], (4, VD), f) * 0.2, 'wfa': jax.random.normal(ks[7], (D, LOW), f) * s, 'wfb': jax.random.normal(ks[8], (LOW, H), f) * s, 'wb': jax.random.normal(ks[9], (D, H), f) * s, 'wga': jax.random.normal(ks[10], (D, LOW), f) * s, 'wgb': jax.random.normal(ks[11], (LOW, VD), f) * s, 'a_log': jax.random.normal(ks[12], (H,), f) * 0.1, 'dt_bias': jnp.ones((H,), f), 'o_norm_w': jnp.ones((DV,), f), 'wo': jax.random.normal(ks[13], (VD, D), f) * s, 'ln1_w': jnp.ones((D,), f), 'ln2_w': jnp.ones((D,), f), 'w_gate': jax.random.normal(ks[14], (D, I), f) * s, 'w_up': jax.random.normal(ks[15], (D, I), f) * s, 'w_down': jax.random.normal(ks[16], (I, D), f) * s}
    _L0_attn_all = _L0_attn_setup()
    _L0_attn_in = {k: v for k, v in _L0_attn_all.items() if k in ('wq', 'wk', 'wv', 'conv_q', 'conv_k', 'conv_v', 'wfa', 'wfb', 'wb', 'wga', 'wgb', 'a_log', 'dt_bias', 'o_norm_w', 'wo', 'ln1_w', 'ln2_w', 'w_gate', 'w_up', 'w_down')}
    del _L0_attn_all

    def _L0_xattn_setup():
        import jax, jax.numpy as jnp
        import numpy as np
        N_HEAD = 8
        key = jax.random.key(seed)
        k1, k2, k3 = jax.random.split(key, 3)
        B, D, L = (4, 128, 256)
        q = jax.random.normal(k1, (B, D, L), dtype=jnp.float32)
        k = jax.random.normal(k2, (B, D, L), dtype=jnp.float32)
        v = jax.random.normal(k3, (B, D, L), dtype=jnp.float32)
        gamma = jnp.ones((), dtype=jnp.float32)
        return {'q': q, 'k': k, 'v': v, 'gamma': gamma}
    _L0_xattn_all = _L0_xattn_setup()
    _L0_xattn_in = {k: v for k, v in _L0_xattn_all.items() if k in ('gamma',)}
    del _L0_xattn_all

    def _L0_ffn_setup():
        import jax, jax.numpy as jnp
        import numpy as np
        E = 64
        K = 4
        H = 256
        I = 192
        C = 32
        B, S = (1, 256)
        key = jax.random.key(seed)
        ks = jax.random.split(key, 8)
        sh = 1.0 / np.sqrt(H).astype(np.float32)
        si = 1.0 / np.sqrt(I).astype(np.float32)
        return {'x': jax.random.normal(ks[0], (B, S, H), jnp.float32), 'w_router': jax.random.normal(ks[1], (E, H), jnp.float32) * sh, 'w_gate': jax.random.normal(ks[2], (E, H, I), jnp.float32) * sh, 'w_up': jax.random.normal(ks[3], (E, H, I), jnp.float32) * sh, 'w_down': jax.random.normal(ks[4], (E, I, H), jnp.float32) * si, 'w_sh_gate': jax.random.normal(ks[5], (H, I), jnp.float32) * sh, 'w_sh_up': jax.random.normal(ks[6], (H, I), jnp.float32) * sh, 'w_sh_down': jax.random.normal(ks[7], (I, H), jnp.float32) * si}
    _L0_ffn_all = _L0_ffn_setup()
    _L0_ffn_in = {k: v for k, v in _L0_ffn_all.items() if k in ('w_router', 'w_gate', 'w_up', 'w_down', 'w_sh_gate', 'w_sh_up', 'w_sh_down')}
    del _L0_ffn_all
    return {'x': x, 'ctx_2048': ctx_2048, 'L0_attn_wq': _L0_attn_in['wq'], 'L0_attn_wk': _L0_attn_in['wk'], 'L0_attn_wv': _L0_attn_in['wv'], 'L0_attn_conv_q': _L0_attn_in['conv_q'], 'L0_attn_conv_k': _L0_attn_in['conv_k'], 'L0_attn_conv_v': _L0_attn_in['conv_v'], 'L0_attn_wfa': _L0_attn_in['wfa'], 'L0_attn_wfb': _L0_attn_in['wfb'], 'L0_attn_wb': _L0_attn_in['wb'], 'L0_attn_wga': _L0_attn_in['wga'], 'L0_attn_wgb': _L0_attn_in['wgb'], 'L0_attn_a_log': _L0_attn_in['a_log'], 'L0_attn_dt_bias': _L0_attn_in['dt_bias'], 'L0_attn_o_norm_w': _L0_attn_in['o_norm_w'], 'L0_attn_wo': _L0_attn_in['wo'], 'L0_attn_ln1_w': _L0_attn_in['ln1_w'], 'L0_attn_ln2_w': _L0_attn_in['ln2_w'], 'L0_attn_w_gate': _L0_attn_in['w_gate'], 'L0_attn_w_up': _L0_attn_in['w_up'], 'L0_attn_w_down': _L0_attn_in['w_down'], 'L0_xattn_gamma': _L0_xattn_in['gamma'], 'L0_ffn_w_router': _L0_ffn_in['w_router'], 'L0_ffn_w_gate': _L0_ffn_in['w_gate'], 'L0_ffn_w_up': _L0_ffn_in['w_up'], 'L0_ffn_w_down': _L0_ffn_in['w_down'], 'L0_ffn_w_sh_gate': _L0_ffn_in['w_sh_gate'], 'L0_ffn_w_sh_up': _L0_ffn_in['w_sh_up'], 'L0_ffn_w_sh_down': _L0_ffn_in['w_sh_down']}

def reference(x, ctx_2048, L0_attn_wq, L0_attn_wk, L0_attn_wv, L0_attn_conv_q, L0_attn_conv_k, L0_attn_conv_v, L0_attn_wfa, L0_attn_wfb, L0_attn_wb, L0_attn_wga, L0_attn_wgb, L0_attn_a_log, L0_attn_dt_bias, L0_attn_o_norm_w, L0_attn_wo, L0_attn_ln1_w, L0_attn_ln2_w, L0_attn_w_gate, L0_attn_w_up, L0_attn_w_down, L0_xattn_gamma, L0_ffn_w_router, L0_ffn_w_gate, L0_ffn_w_up, L0_ffn_w_down, L0_ffn_w_sh_gate, L0_ffn_w_sh_up, L0_ffn_w_sh_down):
    import jax
    import jax.numpy as jnp

    def _L0_attn_ref(x, wq, wk, wv, conv_q, conv_k, conv_v, wfa, wfb, wb, wga, wgb, a_log, dt_bias, o_norm_w, wo, ln1_w, ln2_w, w_gate, w_up, w_down):
        import jax, jax.numpy as jnp
        import numpy as np
        H, DK, DV = (16, 128, 128)
        EPS = 1e-06

        def _causal_dw_conv(x, w):
            K = w.shape[0]
            T = x.shape[1]
            xp = jnp.pad(x, ((0, 0), (K - 1, 0), (0, 0)))
            out = w[0] * xp[:, 0:T, :]
            for i in range(1, K):
                out = out + w[i] * xp[:, i:i + T, :]
            return out

        def _rmsnorm(h, w):
            hf = h.astype(jnp.float32)
            var = jnp.mean(hf * hf, axis=-1, keepdims=True)
            return (hf * jax.lax.rsqrt(var + EPS)).astype(h.dtype) * w

        def _l2norm(x):
            return x * jax.lax.rsqrt(jnp.sum(x * x, axis=-1, keepdims=True) + EPS)
        B, T, D = x.shape
        h = _rmsnorm(x, ln1_w)
        q = jax.nn.silu(_causal_dw_conv(h @ wq, conv_q)).reshape(B, T, H, DK)
        k = jax.nn.silu(_causal_dw_conv(h @ wk, conv_k)).reshape(B, T, H, DK)
        v = jax.nn.silu(_causal_dw_conv(h @ wv, conv_v)).reshape(B, T, H, DV)
        q = _l2norm(q) * DK ** (-0.5)
        k = _l2norm(k)
        g = -jnp.exp(a_log) * jax.nn.softplus(h @ wfa @ wfb + dt_bias)
        beta = jax.nn.sigmoid(h @ wb)

        def step(S, inp):
            qt, kt, vt, gt, bt = inp
            S = S * jnp.exp(gt)[..., None, None]
            kS = jnp.einsum('bhk,bhkv->bhv', kt, S)
            S = S + bt[..., None, None] * (kt[..., :, None] * (vt - kS)[..., None, :])
            ot = jnp.einsum('bhk,bhkv->bhv', qt, S)
            return (S, ot)
        S0 = jnp.zeros((B, H, DK, DV), x.dtype)
        xs = (q.transpose(1, 0, 2, 3), k.transpose(1, 0, 2, 3), v.transpose(1, 0, 2, 3), g.transpose(1, 0, 2), beta.transpose(1, 0, 2))
        _, o = jax.lax.scan(step, S0, xs)
        o = o.transpose(1, 0, 2, 3)
        gate = (h @ wga @ wgb).reshape(B, T, H, DV)
        o = _rmsnorm(o, o_norm_w) * jax.nn.silu(gate.astype(jnp.float32))
        o = o.astype(x.dtype).reshape(B, T, H * DV) @ wo
        x = x + o
        h2 = _rmsnorm(x, ln2_w)
        mlp = jax.nn.silu(h2 @ w_gate) * (h2 @ w_up) @ w_down
        return x + mlp

    def _L0_xattn_ref(q, k, v, gamma):
        import jax, jax.numpy as jnp
        import numpy as np
        N_HEAD = 8
        B, Dq, Lq = q.shape
        Dv, Lk = (v.shape[-2], v.shape[-1])
        h = N_HEAD
        dq = Dq // h
        dv = Dv // h
        qh = q.reshape(B, h, dq, Lq)
        kh = k.reshape(B, h, dq, Lk)
        vh = v.reshape(B, h, dv, Lk)
        scale = 1.0 / jnp.sqrt(jnp.asarray(dq, dtype=q.dtype))
        qk = jnp.einsum('bhdq,bhdl->bhql', qh, kh) * scale
        sm = jax.nn.softmax(qk, axis=-1)
        ret = jnp.einsum('bhql,bhdl->bhdq', sm, vh)
        ret = ret.reshape(B, Dv, Lq)
        return gamma * ret

    def _L0_ffn_ref(x, w_router, w_gate, w_up, w_down, w_sh_gate, w_sh_up, w_sh_down):
        import jax, jax.numpy as jnp
        import numpy as np
        E = 64
        K = 4
        H = 256
        I = 192
        C = 32
        B, S = (1, 256)
        b, s, h = x.shape
        xf = x.reshape(-1, h)
        T = xf.shape[0]
        P = T * K
        logits = xf @ w_router.T
        top_vals, top_idx = jax.lax.top_k(logits, K)
        w_tok = jax.nn.softmax(top_vals.astype(jnp.float32), axis=-1)
        e_flat = top_idx.reshape(-1)
        tok_flat = jnp.repeat(jnp.arange(T), K)
        w_flat = w_tok.reshape(-1)
        order = jnp.argsort(e_flat)
        tok_s = tok_flat[order]
        w_s = w_flat[order]
        counts = jnp.zeros((E,), jnp.int32).at[e_flat].add(1)
        offsets = jnp.cumsum(counts) - counts
        pos = offsets[:, None] + jnp.arange(C)[None, :]
        valid = jnp.arange(C)[None, :] < counts[:, None]
        pos_c = jnp.clip(pos, 0, P - 1)
        tok_ec = tok_s[pos_c]
        w_ec = jnp.where(valid, w_s[pos_c], 0.0)
        x_ec = xf[tok_ec]
        g = jax.nn.silu(jnp.einsum('ech,ehi->eci', x_ec, w_gate))
        u = jnp.einsum('ech,ehi->eci', x_ec, w_up)
        y = jnp.einsum('eci,eih->ech', g * u, w_down)
        contrib = (y * w_ec[..., None]).reshape(-1, h)
        combined = jnp.zeros_like(xf).at[tok_ec.reshape(-1)].add(contrib)
        sg = jax.nn.silu(xf @ w_sh_gate)
        su = xf @ w_sh_up
        combined = combined + sg * su @ w_sh_down
        return combined.reshape(b, s, h)
    x = x + _L0_attn_ref(_layernorm(x, axis=-1), L0_attn_wq, L0_attn_wk, L0_attn_wv, L0_attn_conv_q, L0_attn_conv_k, L0_attn_conv_v, L0_attn_wfa, L0_attn_wfb, L0_attn_wb, L0_attn_wga, L0_attn_wgb, L0_attn_a_log, L0_attn_dt_bias, L0_attn_o_norm_w, L0_attn_wo, L0_attn_ln1_w, L0_attn_ln2_w, L0_attn_w_gate, L0_attn_w_up, L0_attn_w_down)
    x = x + _L0_xattn_ref(_layernorm(x, axis=-1), ctx_2048, ctx_2048, L0_xattn_gamma)
    x = x + _L0_ffn_ref(_layernorm(x, axis=-1), L0_ffn_w_router, L0_ffn_w_gate, L0_ffn_w_up, L0_ffn_w_down, L0_ffn_w_sh_gate, L0_ffn_w_sh_up, L0_ffn_w_sh_down)
    return x

_drawn_inputs = setup_inputs


def setup_inputs(seed=0):
    import zlib

    import numpy as np

    out = dict(_drawn_inputs(seed))
    spreads = {'L0_attn_dt_bias': (1.0, 0.6),
     'L0_attn_o_norm_w': (1.0, 0.6),
     'L0_attn_ln1_w': (1.0, 0.6),
     'L0_attn_ln2_w': (1.0, 0.6)}
    factors = {'L0_attn_wq': 6.147,
     'L0_attn_wk': 7.644,
     'L0_attn_wv': 6.931,
     'L0_attn_conv_q': 6.693,
     'L0_attn_conv_k': 7.563,
     'L0_attn_conv_v': 6.837,
     'L0_attn_wfa': 8.0,
     'L0_attn_wfb': 8.0,
     'L0_attn_wb': 8.0,
     'L0_attn_wga': 5.427,
     'L0_attn_wgb': 5.407,
     'L0_attn_a_log': 8.0,
     'L0_attn_wo': 5.997,
     'ctx_2048': 3.941,
     'L0_attn_w_gate': 8.0,
     'L0_attn_w_up': 8.0,
     'L0_attn_w_down': 8.0,
     'L0_ffn_w_router': 4.233,
     'L0_ffn_w_gate': 4.379,
     'L0_ffn_w_up': 4.081,
     'L0_ffn_w_down': 4.091,
     'L0_ffn_w_sh_gate': 6.396,
     'L0_ffn_w_sh_up': 5.913,
     'L0_ffn_w_sh_down': 5.925}
    for name, (base, spread) in spreads.items():
        noise = np.random.default_rng([zlib.crc32(name.encode()), seed]).standard_normal(out[name].shape)
        drawn = base * np.exp(spread * noise) if base else spread * noise
        out[name] = jnp.asarray(drawn.astype(out[name].dtype))
    for name, factor in factors.items():
        out[name] = (out[name] * factor).astype(out[name].dtype)
    return out
```

```python
from contextlib import ExitStack

import concourse.bass as bass
from concourse import mybir

ACT = mybir.ActivationFunctionType
ALU = mybir.AluOpType
F32 = mybir.dt.float32
BF16 = mybir.dt.bfloat16
U32 = mybir.dt.uint32
AX_X = mybir.AxisListType.X

P = 128
B = 8
D = 256
KD = D // P
TOK = B * P
H = 16
HALF = TOK // 2
LV = 6
I1 = 1024
NI = I1 // P
XH = 8
XD = P // XH
E = 64
K4 = 4
C = 32
SLOTS = E * C
I2 = 192
IH = I2 // 2
GRP = P // C
NG = E // GRP
RING = 4
QB = 32
NQ = P // QB

CONST = {}
_at = 0
for _name, _n in (("ident", P), ("incl", P), ("strict", P), ("level", LV * P), ("identc", QB), ("level0", QB),
                  ("diag", P), ("off5", P), ("negoff5", P), ("ones", P), ("iota", E), ("before", P), ("evenodd", 2)):
    CONST[_name] = (_at, _at + _n)
    _at += _n
NCONST = _at

HT_CONV, HT_G, HT_SB, HT = 0, 12, 12 + B, 12 + 2 * B


def constant_table(np):
    r = np.arange(P)[:, None]
    c = np.arange(P)[None, :]
    j = np.arange(QB)[None, :]
    t = np.zeros((P, NCONST), np.float32)

    def put(name, v):
        a, b = CONST[name]
        t[:, a:b] = v

    put("ident", r == c)
    put("incl", r <= c)
    put("strict", r > c)
    put("before", r < c)
    put("level", np.concatenate([((r >> (k + 1)) == (c >> (k + 1))) & ((c >> k) % 2 == 1) & ((r >> k) % 2 == 0)
                                 for k in range(1, LV + 1)], axis=1))
    put("identc", (r % QB) == j)
    put("level0", ((r % QB) // 2 == j // 2) & (j % 2 == 1) & (r % 2 == 0))
    put("diag", r // QB == c // QB)
    put("off5", ((r // QB) % 2 == 1) & (c // QB == r // QB - 1))
    put("negoff5", -1.0 * (((r // QB) % 2 == 0) & (c // QB == r // QB + 1)))
    put("ones", 1.0)
    put("iota", np.arange(E)[None, :])
    put("evenodd", np.concatenate([(r // XD) % 2 == 0, (r // XD) % 2 == 1], axis=1))
    return t


def need(eng, sem, count):
    if not isinstance(count, int) or count > 0:
        eng.wait_ge(sem, count)


def clear_semaphores(nc, sems):
    numbers = sorted(s.num for s in sems)
    runs, start = [], 0
    for i in range(1, len(numbers) + 1):
        if i == len(numbers) or numbers[i] != numbers[i - 1] + 1:
            runs.append(range(numbers[start], numbers[i - 1] + 1))
            start = i
    with nc.Block() as block:
        @block.sync
        def _(sp):
            for run in runs:
                sp.sem_clear(run)


class Room:

    def __init__(self, arena, start):
        self.arena, self.at = arena, start

    def take(self, *shape):
        n = 1
        for s in shape:
            n *= s
        v = self.arena[:, self.at:self.at + n]
        self.at += n
        assert self.at <= self.arena.shape[1], self.at
        if len(shape) == 2:
            v = v.rearrange("p (a b) -> p a b", b=shape[1])
        elif len(shape) == 3:
            v = v.rearrange("p (a b c) -> p a b c", b=shape[1], c=shape[2])
        elif len(shape) == 4:
            v = v.rearrange("p (a b c d) -> p a b c d", b=shape[1], c=shape[2], d=shape[3])
        return v


def halves(v):
    return v.rearrange("p b t -> p (b t)")


def build_prepare(nc, a, fixed, room, ps):
    x_sb = room.take(B, D)
    hn = room.take(B, D)
    wfa = room.take(KD, P)
    wga = room.take(KD, P)
    wfb = room.take(H)
    wb = room.take(KD, H)
    taps = room.take(3, P)
    ln1 = room.take(KD)
    alog = room.take(H)
    dtb = room.take(H)
    ea = room.take(H)
    lowf = room.take(TOK)
    stats = room.take(B, 6)
    mv = room.take(B, 2)
    sm = room.take(6, B)
    spt, sp1, spr = room.take(B, H), room.take(B, H), room.take(B, H)
    sgm = room.take(B, H)
    cexp = room.take(4)
    consts, x0, hT, lowg, heads = fixed["consts"], fixed["x0"], fixed["hT"], fixed["lowg"], fixed["heads"]

    def const(name):
        return consts[:, CONST[name][0]:CONST[name][1]]

    hps = ps[:, 0:2 * TOK].rearrange("p (k n) -> p k n", k=KD)
    tps = ps[:, 4 * HALF:4 * HALF + 3 * 64].rearrange("p (j r) -> p j r", j=3)
    fps = ps[:, 5 * HALF:7 * HALF]
    gps = ps[:, 0:TOK]
    zps = ps[:, 7 * HALF:7 * HALF + 2 * B * H].rearrange("p (s b h) -> p s b h", s=2, b=B)

    made = []
    with ExitStack() as ctx:
        def sem(name):
            made.append(ctx.enter_context(nc.semaphore(name)))
            return made[-1]

        x_in, w_in, c_in = sem("x_in"), sem("w_in"), sem("c_in")
        stat_made, rstd_made, h_made = sem("stat_made"), sem("rstd_made"), sem("h_made")
        hT_done, hT_made, taps_done = sem("hT_done"), sem("hT_made"), sem("taps_done")
        taps_made, lowf_done, lowf_made, small_done = sem("taps_made"), sem("lowf_done"), sem("lowf_made"), sem("small_done")
        lowg_done, decay_in, decay_sp, ea_made = sem("lowg_done"), sem("decay_in"), sem("decay_sp"), sem("ea_made")
        beta_made, pool_step, vec_step, act_step = sem("beta_made"), sem("pool_step"), sem("vec_step"), sem("act_step")
        block = ctx.enter_context(nc.Block())

        @block.sync
        def _(sp):
            sp.dma_start(x_sb, a["x"].rearrange("b t d -> t b d")).then_inc(x_in, 16)
            sp.dma_start(consts, a["consts"]).then_inc(c_in, 16)
            for dst, src in ((wfa, a["wfa"]), (wga, a["wga"]), (wb, a["wb"])):
                sp.dma_start(dst, src.rearrange("(k p) n -> p k n", p=P)).then_inc(w_in, 16)
            sp.dma_start(wfb, a["wfb"]).then_inc(w_in, 16)
            for j, name in enumerate(("conv_q", "conv_k", "conv_v")):
                sp.dma_start(taps[0:64, j, :], a[name].rearrange("i (h c) -> (i h) c", c=P)).then_inc(w_in, 16)
            sp.dma_start(alog, a["a_log"].partition_broadcast(P)).then_inc(w_in, 16)
            sp.dma_start(dtb, a["dt_bias"].partition_broadcast(P)).then_inc(w_in, 16)
            with nc.allow_non_contiguous_dma(reason="256 single weights, feature on partition"):
                for k in range(KD):
                    sp.dma_start(ln1[:, k:k + 1], a["ln1_w"].rearrange("(k p o) -> k p o", p=P, o=1)[k]).then_inc(w_in, 16)
            sp.dma_start(fixed["onw"], a["o_norm_w"].rearrange("(p o) -> p o", o=1)).then_inc(w_in, 16)
        W_ALL = 16 * 12

        @block.vector
        def _(dve):
            dve.wait_ge(x_in, 16)
            for b in range(B):
                nc.vector.bn_stats(stats[:, b, :], x_sb[:, b, :]).then_inc(vec_step, 1)
            for b in range(B):
                dve.wait_ge(vec_step, b + 1)
                nc.vector.bn_aggr(mv[:, b, :], stats[:, b, :]).then_inc(stat_made, 1)
            dve.wait_ge(rstd_made, 2)
            for b in range(B):
                nc.vector.tensor_scalar(x0[:, b, :], x_sb[:, b, :], mv[:, b, 0:1], sm[:, 0, b:b + 1],
                                        ALU.subtract, ALU.mult)
                nc.vector.tensor_scalar(hn[:, b, :], x_sb[:, b, :], mv[:, b, 0:1], sm[:, 4, b:b + 1],
                                        ALU.subtract, ALU.mult).then_inc(h_made, 1)
            dve.wait_ge(taps_done, 3)
            for j in range(3):
                nc.vector.tensor_copy(heads[:, :, 4 * j:4 * j + 4].rearrange("p h i -> p i h"),
                                      tps[:, j, :].rearrange("p (i h) -> p i h", i=4)).then_inc(taps_made, 1)
            dve.wait_ge(small_done, 1)
            nc.vector.tensor_tensor(spt, zps[:, 0], dtb.unsqueeze(1).broadcast_to([P, B, H]), ALU.add).then_inc(decay_in, 1)
            dve.wait_ge(decay_sp, 1)
            dve.wait_ge(act_step, 3)
            nc.vector.tensor_tensor(spt, sp1, spr, ALU.add).then_inc(vec_step, 1)
            dve.wait_ge(ea_made, 1)
            dve.wait_ge(vec_step, B + 1)
            nc.vector.scalar_tensor_tensor(heads[:, :, HT_G:HT_G + B].rearrange("p h b -> p b h"), spt, -1.0,
                                           ea.unsqueeze(1).broadcast_to([P, B, H]), ALU.mult, ALU.mult)

        @block.gpsimd
        def _(pool):
            nc.gpsimd.memset(cexp[:, 0:1], -0.5).then_inc(pool_step, 1)
            nc.gpsimd.memset(cexp[:, 1:2], 0.5).then_inc(pool_step, 1)
            nc.gpsimd.memset(fixed["mhalf"], -0.5).then_inc(pool_step, 1)
            pool.wait_ge(stat_made, B)
            pool.wait_ge(pool_step, 3)
            var = mv[:, :, 1]
            mh = cexp[:, 0:1].broadcast_to([P, B])
            nc.gpsimd.tensor_scalar(sm[:, 1, :], var, 1e-5, None, ALU.add).then_inc(pool_step, 1)
            pool.wait_ge(pool_step, 4)
            nc.gpsimd.tensor_tensor(sm[:, 0, :], sm[:, 1, :], mh, ALU.pow).then_inc(rstd_made, 1)
            pool.wait_ge(rstd_made, 1)
            nc.gpsimd.tensor_tensor(sm[:, 2, :], var, sm[:, 0, :], ALU.mult).then_inc(pool_step, 1)
            pool.wait_ge(pool_step, 5)
            nc.gpsimd.tensor_tensor(sm[:, 3, :], sm[:, 2, :], sm[:, 0, :], ALU.mult).then_inc(pool_step, 1)
            pool.wait_ge(pool_step, 6)
            nc.gpsimd.tensor_scalar(sm[:, 1, :], sm[:, 3, :], 1e-6, None, ALU.add).then_inc(pool_step, 1)
            pool.wait_ge(pool_step, 7)
            nc.gpsimd.tensor_tensor(sm[:, 5, :], sm[:, 1, :], mh, ALU.pow).then_inc(pool_step, 1)
            pool.wait_ge(pool_step, 8)
            nc.gpsimd.tensor_tensor(sm[:, 4, :], sm[:, 5, :], sm[:, 0, :], ALU.mult).then_inc(rstd_made, 1)
            pool.wait_ge(beta_made, 1)
            nc.gpsimd.tensor_tensor(heads[:, :, HT_SB:HT_SB + B].rearrange("p h b -> p b h"), sgm,
                                    cexp[:, 1:2].unsqueeze(1).broadcast_to([P, B, H]), ALU.pow)

        @block.scalar
        def _(act):
            act.wait_ge(w_in, W_ALL)
            nc.scalar.activation(ea, alog, ACT.Exp).then_inc(ea_made, 1)
            act.wait_ge(hT_done, 1)
            for k in range(KD):
                nc.scalar.activation(hT[:, k, :], hps[:, k, :], ACT.Copy, scale=ln1[:, k:k + 1]).then_inc(hT_made, 1)
            act.wait_ge(lowf_done, 1)
            nc.scalar.activation(lowf, fps, ACT.Copy).then_inc(lowf_made, 1)
            act.wait_ge(lowg_done, 1)
            nc.scalar.activation(lowg, gps, ACT.Copy)
            act.wait_ge(decay_in, 1)
            nc.scalar.activation(sgm, zps[:, 1], ACT.Sigmoid).then_inc(beta_made, 1)
            nc.scalar.activation(sp1, spt, ACT.Abs).then_inc(act_step, 1)
            act.wait_ge(act_step, 1)
            nc.scalar.activation(sp1, sp1, ACT.Exp, scale=-1.0).then_inc(act_step, 1)
            nc.scalar.activation(spr, spt, ACT.Relu).then_inc(act_step, 1)
            act.wait_ge(act_step, 2)
            nc.scalar.activation(sp1, sp1, ACT.Ln, bias=1.0).then_inc(decay_sp, 1)

        @block.tensor
        def _(pe):
            pe.wait_ge(c_in, 16)
            pe.wait_ge(w_in, W_ALL)
            ident = const("ident")
            for j in range(3):
                nc.tensor.transpose(tps[:, j, :], taps[0:64, j, :], ident[0:64, 0:64]).then_inc(taps_done, 1)
            for b in range(B):
                pe.wait_ge(h_made, b + 1)
                for k in range(KD):
                    last = nc.tensor.transpose(hps[:, k, b * P:(b + 1) * P], hn[:, b, k * P:(k + 1) * P], ident)
            last.then_inc(hT_done, 1)
            pe.wait_ge(hT_made, KD)
            for w, dst, done in ((wfa, fps, lowf_done), (wga, gps, lowg_done)):
                for n in range(2):
                    for k in range(KD):
                        last = nc.tensor.matmul(dst[:, n * HALF:(n + 1) * HALF], w[:, k, :],
                                                hT[:, k, n * HALF:(n + 1) * HALF], start=(k == 0), stop=(k == KD - 1))
                last.then_inc(done, 1)
            pe.wait_ge(lowf_made, 1)
            for b in range(B):
                for k in range(KD):
                    nc.tensor.matmul(zps[:, 1, b, :], hT[:, k, b * P:(b + 1) * P], wb[:, k, :],
                                     start=(k == 0), stop=(k == KD - 1))
                last = nc.tensor.matmul(zps[:, 0, b, :], lowf[:, b * P:(b + 1) * P], wfb, start=True, stop=True)
            last.then_inc(small_done, 1)

    return made


def build_delta(nc, a, fixed, room, ps):
    consts, hT, lowg, heads, o_all = fixed["consts"], fixed["hT"], fixed["lowg"], fixed["heads"], fixed["o_all"]
    onw, mhalf = fixed["onw"], fixed["mhalf"]

    def const(name):
        return consts[:, CONST[name][0]:CONST[name][1]]

    ident, incl, ones = const("ident"), const("incl"), const("ones")
    levels = const("level").rearrange("p (k n) -> p k n", k=LV)

    wqkv = room.take(3, KD, P)
    wg = room.take(P)
    small = room.take(HT)
    conv = [room.take(B, P) for _ in range(3)]
    squares = [room.take(B, P) for _ in range(2)]
    gates = [room.take(B, P) for _ in range(2)]
    kp = room.take(B, P)
    dec = room.take(B, P)
    gm = room.take(B, P)
    lt = [room.take(B, P) for _ in range(2)]
    pt = [room.take(B, P) for _ in range(2)]
    vp = [room.take(B, P) for _ in range(2)]
    cmask = [room.take(B, P) for _ in range(3)]
    yx = room.take(B, P)
    zc = room.take(B, QB)
    xc = room.take(B, QB)
    ltc = room.take(B, QB)
    z6 = room.take(B, P)
    t5 = room.take(B, P)
    u = room.take(B, P)
    rr = room.take(B, P)
    og = room.take(B, P)
    osq = room.take(B, P)
    qk_sum = room.take(2 * B)
    o_sum = room.take(B)
    rk = room.take(B)
    rq = [room.take(2, B) for _ in range(2)]
    ro = room.take(B)
    pw = room.take(6, 2 * B)

    pa, pb, pc, pd = [ps[:, 2 * HALF * i:2 * HALF * (i + 1)].rearrange("p (b t) -> p b t", b=B) for i in range(4)]
    sums_ps = ps[:, 2 * HALF:2 * HALF + 2 * B]
    osum_ps = ps[:, 4 * HALF:4 * HALF + B]
    yc = ps[:, 4 * HALF:4 * HALF + B * QB].rearrange("p (b j) -> p b j", b=B)
    dzc = ps[:, 6 * HALF:6 * HALF + B * QB].rearrange("p (b j) -> p b j", b=B)

    def blocks(v):
        return v.unsqueeze(2).broadcast_to([P, B, NQ, QB])

    def four(v):
        return v.rearrange("p b (q j) -> p b q j", q=NQ)

    def over_b(v, n):
        return v.unsqueeze(1).broadcast_to([P, B, n])

    def pattern(name):
        return const(name).rearrange("p (q j) -> p q j", q=NQ).unsqueeze(1).broadcast_to([P, B, NQ, QB])

    made = []
    with ExitStack() as ctx:
        def sem(name):
            made.append(ctx.enter_context(nc.semaphore(name)))
            return made[-1]

        w_in = sem("head_w_in")
        small_made = sem("small_made")
        proj_done = [sem(f"{n}_proj_done") for n in ("q", "k", "v", "gate")]
        tap0_made = [sem(f"{n}_tap0_made") for n in "qkv"]
        conv_made = [sem(f"{n}_conv_made") for n in "qkv"]
        silu_made = [sem(f"{n}_silu_made") for n in ("q", "k", "v", "gate")]
        sq_made = sem("sq_made")
        sums_done, sums_made, rk_made, rkrep_done, kp_made = sem("sums_done"), sem("sums_made"), sem("rk_made"), sem("rkrep_done"), sem("kp_made")
        vt_done, vp_made, gm_made, diff_done = sem("vt_done"), sem("vp_made"), sem("gm_made"), sem("diff_done")
        exp_made, dec_made, kk_done, qk_done = sem("exp_made"), sem("dec_made"), sem("kk_done"), sem("qk_done")
        lt_made, pt_made, cmask_made, ltc_made = sem("lt_made"), sem("pt_made"), sem("cmask_made"), sem("ltc_made")
        z_step = sem("z_step")
        x_made = sem("x_made")
        cx_done, yx_made, dz_done = sem("cx_done"), sem("yx_made"), sem("dz_done")
        zdiag_made, t5_made, z6_made = sem("zdiag_made"), sem("t5_made"), sem("z6_made")
        w_done, w_made, r_made, xr_done, u_made = sem("w_done"), sem("w_made"), sem("r_made"), sem("xr_done"), sem("u_made")
        o_done, og_made, osq_made, osum_done, osum_made = sem("o_done"), sem("og_made"), sem("osq_made"), sem("osum_done"), sem("osum_made")
        ro_made, rorep_done, head_made, pool_step = sem("ro_made"), sem("rorep_done"), sem("head_made"), sem("norm_step")
        block = ctx.enter_context(nc.Block())

        def all_heads(eng, body):
            body(-1, 1, False, True)
            body(0, 0, True, True)
            body(1, 1, True, True)
            with eng.Fori(1, (H - 2) // 2) as i:
                body(i * 2, 0, True, True)
                body(i * 2 + 1, 1, True, True)
            body(H - 2, 0, True, True)
            body(H - 1, 1, True, False)

        @block.sync
        def _(sp):
            def body(f):
                need(sp, proj_done[3], f)
                sp.nop(nofuse=True)
                for j, name in enumerate(("wq", "wk", "wv")):
                    sp.dma_start(wqkv[:, j], a[name].rearrange("(k p) (h c) -> h p k c", p=P, c=P)[f]).then_inc(w_in, 16)
                sp.dma_start(wg, a["wgb"].rearrange("p (h c) -> h p c", c=P)[f]).then_inc(w_in, 16)
            body(0)
            with sp.Fori(1, H) as f:
                body(f)

        @block.tensor
        def _(pe):
            def project(j, f, n):
                dst = (pa, pb, pa, pb)[j]
                if j < 3:
                    for k in range(KD):
                        last = nc.tensor.matmul(halves(dst)[:, n * HALF:(n + 1) * HALF], wqkv[:, j, k, :],
                                                hT[:, k, n * HALF:(n + 1) * HALF], start=(k == 0), stop=(k == KD - 1))
                else:
                    last = nc.tensor.matmul(halves(dst)[:, n * HALF:(n + 1) * HALF], wg,
                                            lowg[:, n * HALF:(n + 1) * HALF], start=True, stop=True)
                if n == 1:
                    last.then_inc(proj_done[j], 1)

            def each(dst, lhs, rhs, done):
                for b in range(B):
                    last = nc.tensor.matmul(dst[:, b, :], lhs(b), rhs(b), start=True, stop=True)
                last.then_inc(done, 1)

            def body(h, par, back, front):
                f = h + 1
                fpar = 1 - par

                def cx(k):
                    pe.wait_ge(x_made, 5 * h + k)
                    pe.wait_ge(cmask_made, LV * h + k)
                    each(yc, lambda b: cmask[(k - 1) % 3][:, b, :], lambda b: xc[:, b, :], cx_done)

                def dz(k):
                    if k == 1:
                        need(pe, head_made, h)
                    pe.wait_ge(yx_made, 5 * h + k)
                    each(dzc, lambda b: yx[:, b, :], lambda b: zc[:, b, :], dz_done)

                if back:
                    cx(1)
                if front:
                    pe.wait_ge(w_in, 64 * f + 64)
                    need(pe, lt_made, f)
                    project(0, f, 0)
                if back:
                    dz(1)
                if front:
                    project(0, f, 1)
                if back:
                    cx(2)
                if front:
                    need(pe, pt_made, f)
                    project(1, f, 0)
                if back:
                    dz(2)
                if front:
                    project(1, f, 1)
                if back:
                    cx(3)
                if front:
                    pe.wait_ge(conv_made[0], 3 * f + 3)
                    project(2, f, 0)
                if back:
                    dz(3)
                if front:
                    project(2, f, 1)
                if back:
                    cx(4)
                if front:
                    pe.wait_ge(conv_made[1], 3 * f + 3)
                    project(3, f, 0)
                if back:
                    dz(4)
                if front:
                    project(3, f, 1)
                if back:
                    cx(5)
                if front:
                    pe.wait_ge(silu_made[2], f + 1)
                    for b in range(B):
                        last = nc.tensor.transpose(pa[:, b, :], conv[2][:, b, :], ident)
                    last.then_inc(vt_done, 1)
                if back:
                    dz(5)
                if front:
                    pe.wait_ge(silu_made[3], f + 1)
                    pe.wait_ge(sq_made, 2 * f + 2)
                    for j, sq in enumerate((squares[1], squares[0])):
                        for b in range(B):
                            last = nc.tensor.matmul(sums_ps[:, j * B + b:j * B + b + 1], sq[:, b, :], ones[:, 0:1],
                                                    start=True, stop=True)
                    last.then_inc(sums_done, 1)
                if back:
                    pe.wait_ge(z6_made, h + 1)
                    each(pc, lambda b: z6[:, b, :], lambda b: vp[par][:, b, :], w_done)
                if front:
                    pe.wait_ge(vp_made, f + 1)
                    pe.wait_ge(gm_made, f + 1)
                    for n in range(2):
                        last = nc.tensor.matmul(halves(pa)[:, n * HALF:(n + 1) * HALF], const("strict"),
                                                halves(gm)[:, n * HALF:(n + 1) * HALF], start=True, stop=True)
                    last.then_inc(diff_done, 1)
                if back:
                    pe.wait_ge(w_made, h + 1)
                    pe.wait_ge(cmask_made, LV * h + LV)
                    each(pd, lambda b: cmask[(LV - 1) % 3][:, b, :], lambda b: u[:, b, :], cx_done)
                if front:
                    pe.wait_ge(rk_made, f + 1)
                    each(pb, lambda b: rk[:, b:b + 1].broadcast_to([P, P]), lambda b: ident, rkrep_done)
                if back:
                    pe.wait_ge(r_made, h + 1)
                    each(pc, lambda b: z6[:, b, :], lambda b: rr[:, b, :], xr_done)
                if front:
                    pe.wait_ge(kp_made, f + 1)
                    pe.wait_ge(exp_made, f + 1)
                    each(pa, lambda b: kp[:, b, :], lambda b: kp[:, b, :], kk_done)
                    each(pb, lambda b: kp[:, b, :], lambda b: conv[0][:, b, :], qk_done)
                if back:
                    pe.wait_ge(u_made, h + 1)
                    each(pd, lambda b: u[:, b, :], lambda b: pt[par][:, b, :], o_done)
                    pe.wait_ge(osq_made, h + 1)
                    for b in range(B):
                        last = nc.tensor.matmul(osum_ps[:, b:b + 1], osq[:, b, :], ones[:, 0:1], start=True, stop=True)
                    last.then_inc(osum_done, 1)
                    pe.wait_ge(og_made, h + 1)
                    pe.wait_ge(ro_made, h + 1)
                    each(pd, lambda b: ro[:, b:b + 1].broadcast_to([P, P]), lambda b: ident, rorep_done)

            all_heads(pe, body)

        @block.scalar
        def _(act):
            def tap0(j, f):
                act.wait_ge(proj_done[j], f + 1)
                act.wait_ge(small_made, f + 1)
                need(act, (qk_done, kp_made, vt_done)[j], f)
                nc.scalar.activation(halves(conv[j]), halves((pa, pb, pa)[j]), ACT.Copy,
                                     scale=small[:, 4 * j + 3:4 * j + 4]).then_inc(tap0_made[j], 1)

            def silu(j, f):
                act.wait_ge(conv_made[j], 3 * f + 3)
                nc.scalar.activation(halves(conv[j]), halves(conv[j]), ACT.Silu).then_inc(silu_made[j], 1)

            def square(j, f):
                act.wait_ge(silu_made[j], f + 1)
                need(act, sums_done, f)
                nc.scalar.activation(halves(squares[j]), halves(conv[j]), ACT.Square).then_inc(sq_made, 1)

            def body(h, par, back, front):
                f = h + 1
                fpar = 1 - par
                if back:
                    act.wait_ge(lt_made, h + 1)
                    need(act, x_made, 5 * h)
                    for q in range(NQ):
                        s = slice(q * QB, (q + 1) * QB)
                        last = nc.scalar.activation(ltc[s], lt[par][s, :, s], ACT.Copy)
                    last.then_inc(ltc_made, 1)
                if front:
                    tap0(0, f)
                    tap0(1, f)
                    silu(0, f)
                    tap0(2, f)
                    square(0, f)
                    silu(1, f)
                    square(1, f)
                    silu(2, f)
                    act.wait_ge(proj_done[3], f + 1)
                    nc.scalar.activation(halves(gates[fpar]), halves(pb), ACT.Silu).then_inc(silu_made[3], 1)
                if back:
                    act.wait_ge(w_done, h + 1)
                    nc.scalar.activation(halves(u), halves(pc), ACT.Copy).then_inc(w_made, 1)
                if front:
                    act.wait_ge(diff_done, f + 1)
                    need(act, pt_made, f)
                    nc.scalar.activation(halves(dec), halves(pa), ACT.Exp).then_inc(exp_made, 1)
                if back:
                    act.wait_ge(cx_done, LV * h + LV)
                    nc.scalar.activation(halves(rr), halves(pd), ACT.Copy).then_inc(r_made, 1)
                    act.wait_ge(o_done, h + 1)
                    nc.scalar.activation(halves(osq), halves(pd), ACT.Square).then_inc(osq_made, 1)

            all_heads(act, body)

        @block.vector
        def _(dve):
            def tap(j, f, shift):
                if shift == 1:
                    dve.wait_ge(tap0_made[j], f + 1)
                else:
                    dve.wait_ge(conv_made[j], 3 * f + shift - 1)
                nc.vector.scalar_tensor_tensor(conv[j][:, :, shift:], (pa, pb, pa)[j][:, :, :P - shift],
                                               small[:, 4 * j + 3 - shift:4 * j + 4 - shift], conv[j][:, :, shift:],
                                               ALU.mult, ALU.add).then_inc(conv_made[j], 1)

            def body(h, par, back, front):
                f = h + 1
                fpar = 1 - par

                def to_x(k, steps):
                    dve.wait_ge(z_step, 6 * h + steps)
                    nc.vector.transpose(xc.rearrange("p b j -> p (b j)"), zc.rearrange("p b j -> p (b j)")).then_inc(x_made, 1)

                def expand(k):
                    dve.wait_ge(cx_done, LV * h + k)
                    nc.vector.tensor_tensor(four(yx), blocks(yc), pattern("off5" if k == 5 else "diag"),
                                            ALU.mult).then_inc(yx_made, 1)

                def update(k):
                    dve.wait_ge(dz_done, 5 * h + k)
                    nc.vector.tensor_tensor(zc, zc, dzc, ALU.subtract).then_inc(z_step, 1)
                    to_x(k + 1, 2 + k)

                if back:
                    dve.wait_ge(ltc_made, h + 1)
                    need(dve, zdiag_made, h)
                    nc.vector.tensor_tensor(zc, ltc, over_b(const("level0"), QB), ALU.mult).then_inc(z_step, 1)
                    dve.wait_ge(z_step, 6 * h + 1)
                    nc.vector.tensor_tensor(zc, over_b(const("identc"), QB), zc, ALU.subtract).then_inc(z_step, 1)
                    to_x(1, 2)
                    expand(1)
                if front:
                    dve.wait_ge(small_made, f + 1)
                    tap(0, f, 1)
                if back:
                    update(1)
                if front:
                    tap(0, f, 2)
                if back:
                    expand(2)
                if front:
                    tap(0, f, 3)
                if back:
                    update(2)
                if front:
                    tap(1, f, 1)
                if back:
                    expand(3)
                if front:
                    tap(1, f, 2)
                    tap(1, f, 3)
                if back:
                    update(3)
                if front:
                    tap(2, f, 1)
                if back:
                    expand(4)
                if front:
                    tap(2, f, 2)
                    tap(2, f, 3)
                if back:
                    update(4)
                    expand(5)
                if front:
                    dve.wait_ge(vt_done, f + 1)
                    nc.vector.tensor_tensor(vp[fpar], pa, small[:, HT_SB:HT_SB + B].unsqueeze(2).broadcast_to([P, B, P]),
                                            ALU.mult).then_inc(vp_made, 1)
                if back:
                    dve.wait_ge(dz_done, 5 * h + 5)
                    nc.vector.tensor_tensor(four(t5), blocks(dzc), pattern("negoff5"), ALU.mult).then_inc(t5_made, 1)
                    dve.wait_ge(t5_made, h + 1)
                    dve.wait_ge(zdiag_made, h + 1)
                    nc.vector.tensor_tensor(halves(z6), halves(z6), halves(t5), ALU.add).then_inc(z6_made, 1)
                if front:
                    dve.wait_ge(sums_done, f + 1)
                    nc.vector.tensor_copy(qk_sum, sums_ps).then_inc(sums_made, 1)
                    dve.wait_ge(rkrep_done, f + 1)
                    nc.vector.tensor_tensor(halves(kp), halves(conv[1]), halves(pb), ALU.mult).then_inc(kp_made, 1)
                if back:
                    dve.wait_ge(xr_done, h + 1)
                    nc.vector.tensor_tensor(halves(u), halves(u), halves(pc), ALU.subtract).then_inc(u_made, 1)
                if front:
                    dve.wait_ge(kk_done, f + 1)
                    dve.wait_ge(dec_made, f + 1)
                    if not (isinstance(f, int) and f < 2):
                        dve.wait_ge(cmask_made, LV * (f - 1))
                        dve.wait_ge(ltc_made, f - 1)
                    nc.vector.tensor_tensor(halves(lt[fpar]), halves(pa), halves(dec), ALU.mult).then_inc(lt_made, 1)
                    dve.wait_ge(qk_done, f + 1)
                    nc.vector.tensor_tensor(halves(pt[fpar]), halves(pb), halves(dec), ALU.mult).then_inc(pt_made, 1)
                if back:
                    dve.wait_ge(osq_made, h + 1)
                    nc.vector.scalar_tensor_tensor(halves(og), halves(pd), onw, halves(gates[par]),
                                                   ALU.mult, ALU.mult).then_inc(og_made, 1)
                    dve.wait_ge(osum_done, h + 1)
                    nc.vector.tensor_copy(o_sum, osum_ps).then_inc(osum_made, 1)
                    dve.wait_ge(rorep_done, h + 1)
                    nc.vector.tensor_tensor(o_all[:, h, :], halves(og), halves(pd), ALU.mult).then_inc(head_made, 1)

            all_heads(dve, body)

        @block.gpsimd
        def _(pool):
            mh = mhalf.broadcast_to([P, 2 * B])
            steps = [0]

            def body(h, par, back, front):
                f = h + 1
                fpar = 1 - par

                def mask(k):
                    if k > 3:
                        pool.wait_ge(cx_done, LV * h + k - 3)
                    nc.gpsimd.tensor_tensor(cmask[(k - 1) % 3], lt[par], over_b(levels[:, k - 1, :], P),
                                            ALU.mult).then_inc(cmask_made, 1)

                if back:
                    pool.wait_ge(lt_made, h + 1)
                    need(pool, xr_done, h)
                    mask(1)
                    mask(2)
                    mask(3)
                if front:
                    need(pool, conv_made[2], 3 * f)
                    need(pool, vp_made, f)
                    pool.nop(nofuse=True)
                    nc.gpsimd.tensor_copy(small, heads[:, f, :]).then_inc(small_made, 1)
                    pool.wait_ge(small_made, f + 1)
                    need(pool, diff_done, f)
                    nc.gpsimd.tensor_tensor(gm, over_b(incl, P), small[:, HT_G:HT_G + B].unsqueeze(2).broadcast_to([P, B, P]),
                                            ALU.mult).then_inc(gm_made, 1)
                if back:
                    mask(4)
                    mask(5)
                    need(pool, xr_done, h)
                    pool.wait_ge(x_made, 5 * h + 5)
                    nc.gpsimd.tensor_tensor(four(z6), blocks(zc), pattern("diag"), ALU.mult).then_inc(zdiag_made, 1)
                    mask(6)
                if front:
                    n = 4 * f
                    pool.wait_ge(sums_made, f + 1)
                    need(pool, rkrep_done, f)
                    pool.nop(nofuse=True)
                    nc.gpsimd.tensor_scalar(pw[:, 0, :], qk_sum, 1e-6, None, ALU.add).then_inc(pool_step, 1)
                    pool.wait_ge(pool_step, n + 1)
                    nc.gpsimd.tensor_tensor(pw[:, 1, :], pw[:, 0, :], mh, ALU.pow).then_inc(pool_step, 1)
                    pool.wait_ge(pool_step, n + 2)
                    nc.gpsimd.tensor_tensor(rk, pw[:, 1, 0:B], small[:, HT_SB:HT_SB + B], ALU.mult).then_inc(rk_made, 1)
                    nc.gpsimd.tensor_scalar(rq[fpar][:, 0, :], pw[:, 1, B:2 * B], float(P) ** -0.5, None, ALU.mult).then_inc(pool_step, 1)
                    pool.wait_ge(pool_step, n + 3)
                    nc.gpsimd.tensor_tensor(rq[fpar][:, 1, :], rq[fpar][:, 0, :], rq[fpar][:, 0, :], ALU.mult).then_inc(pool_step, 1)
                    pool.wait_ge(exp_made, f + 1)
                    nc.gpsimd.tensor_tensor(dec, dec, over_b(incl, P), ALU.mult).then_inc(dec_made, 1)
                if back:
                    pool.wait_ge(osum_made, h + 1)
                    need(pool, rorep_done, h)
                    pool.wait_ge(pool_step, 4 * h + 4)
                    nc.gpsimd.tensor_tensor(pw[:, 2, 0:B], o_sum, rq[par][:, 1, :], ALU.mult).then_inc(norm_o, 1)
                    pool.wait_ge(norm_o, 3 * h + 1)
                    pool.nop(nofuse=True)
                    nc.gpsimd.tensor_scalar(pw[:, 3, 0:B], pw[:, 2, 0:B], 1.0 / P, 1e-6, ALU.mult, ALU.add).then_inc(norm_o, 1)
                    pool.wait_ge(norm_o, 3 * h + 2)
                    nc.gpsimd.tensor_tensor(pw[:, 4, 0:B], pw[:, 3, 0:B], mh[:, 0:B], ALU.pow).then_inc(norm_o, 1)
                    pool.wait_ge(norm_o, 3 * h + 3)
                    nc.gpsimd.tensor_tensor(ro, pw[:, 4, 0:B], rq[par][:, 0, :], ALU.mult).then_inc(ro_made, 1)

            norm_o = sem("onorm_step")
            all_heads(pool, body)

    return made


def build_mlp(nc, a, fixed, room, ps):
    consts, x0, o_all, x1 = fixed["consts"], fixed["x0"], fixed["o_all"], fixed["x1"]
    ident = consts[:, CONST["ident"][0]:CONST["ident"][1]]
    wo = room.take(H, D)
    w_gate = room.take(KD, I1)
    w_up = room.take(KD, I1)
    w_down = room.take(NI, D)
    xr = room.take(B, D)
    xa = room.take(B, D)
    h2 = room.take(B, D)
    sqr = room.take(D)
    h2T = room.take(KD, TOK)
    mT = room.take(NI, TOK)
    sg = [room.take(TOK) for _ in range(2)]
    ln2 = room.take(KD)
    ms, rms = room.take(B), room.take(B)
    tmp = room.take(B)

    with ExitStack() as ctx:
        def sem(name):
            return ctx.enter_context(nc.semaphore(name))

        wo_in, w_in, x_in = sem("wo_in"), sem("mlp_w_in"), sem("x_again_in")
        oproj_done, xa_made, xr_made, ms_made, rms_made = sem("oproj_done"), sem("xa_made"), sem("xr_made"), sem("ms_made"), sem("rms_made")
        h2_made, h2T_done, h2T_made = sem("h2_made"), sem("h2T_done"), sem("h2T_made")
        gate_done, up_done, sg_made, m_made = sem("gate_done"), sem("up_done"), sem("sg_made"), sem("m_made")
        down_done, pool_step = sem("down_done"), sem("rms_step")
        block = ctx.enter_context(nc.Block())

        @block.sync
        def _(sp):
            for part in range(4):
                sp.dma_start(wo[:, 4 * part:4 * part + 4, :],
                             a["wo"].rearrange("(h c) n -> c h n", c=P)[:, 4 * part:4 * part + 4, :]).then_inc(wo_in, 16)
            sp.dma_start(w_gate, a["w_gate"].rearrange("(k p) n -> p k n", p=P)).then_inc(w_in, 16)
            sp.dma_start(w_up, a["w_up"].rearrange("(k p) n -> p k n", p=P)).then_inc(w_in, 16)
            sp.dma_start(w_down, a["w_down"].rearrange("(c p) n -> p c n", p=P)).then_inc(w_in, 16)
            sp.dma_start(xr, a["x"].rearrange("b t d -> t b d")).then_inc(x_in, 16)
            with nc.allow_non_contiguous_dma(reason="256 single weights, feature on partition"):
                for k in range(KD):
                    sp.dma_start(ln2[:, k:k + 1], a["ln2_w"].rearrange("(k p o) -> k p o", p=P, o=1)[k]).then_inc(x_in, 16)

        def tok_cols(b):
            return ps[:, b * D:(b + 1) * D]

        def gate_ps(c):
            return ps[:, (c % 2) * 2 * TOK:(c % 2) * 2 * TOK + TOK]

        def up_ps(c):
            return ps[:, (c % 2) * 2 * TOK + TOK:(c % 2) * 2 * TOK + 2 * TOK]

        hps = ps[:, 2 * TOK:4 * TOK].rearrange("p (k n) -> p k n", k=KD)

        @block.tensor
        def _(pe):
            for b in range(B):
                for h in range(H):
                    if b == 0 and h % 4 == 0:
                        pe.wait_ge(wo_in, 64)
                    last = nc.tensor.matmul(tok_cols(b), o_all[:, h, b * P:(b + 1) * P], wo[:, h, :],
                                            start=(h == 0), stop=(h == H - 1))
                if b % 2:
                    last.then_inc(oproj_done, 1)
            for b in range(B):
                pe.wait_ge(h2_made, b + 1)
                for k in range(KD):
                    last = nc.tensor.transpose(hps[:, k, b * P:(b + 1) * P], h2[:, b, k * P:(k + 1) * P], ident)
            last.then_inc(h2T_done, 1)
            pe.wait_ge(h2T_made, KD)
            pe.wait_ge(w_in, 48)
            for c in range(NI):
                if c >= 2:
                    pe.wait_ge(m_made, c - 1)
                for w, dst, done in ((w_gate, gate_ps(c), gate_done), (w_up, up_ps(c), up_done)):
                    for n in range(2):
                        for k in range(KD):
                            last = nc.tensor.matmul(dst[:, n * HALF:(n + 1) * HALF], w[:, k, c * P:(c + 1) * P],
                                                    h2T[:, k, n * HALF:(n + 1) * HALF], start=(k == 0), stop=(k == KD - 1))
                    last.then_inc(done, 1)
            pe.wait_ge(m_made, NI)
            for b in range(B):
                for c in range(NI):
                    last = nc.tensor.matmul(tok_cols(b), mT[:, c, b * P:(b + 1) * P], w_down[:, c, :],
                                            start=(c == 0), stop=(c == NI - 1))
                if b % 2:
                    last.then_inc(down_done, 1)

        @block.vector
        def _(dve):
            for b in range(B):
                if b % 2 == 0:
                    dve.wait_ge(oproj_done, b // 2 + 1)
                nc.vector.tensor_tensor(xa[:, b, :], x0[:, b, :], tok_cols(b), ALU.add).then_inc(xa_made, 1)
            dve.wait_ge(rms_made, 1)
            for b in range(B):
                nc.vector.tensor_scalar(h2[:, b, :], xa[:, b, :], rms[:, b:b + 1], None, ALU.mult).then_inc(h2_made, 1)
            for c in range(NI):
                dve.wait_ge(sg_made, c + 1)
                dve.wait_ge(up_done, c + 1)
                nc.vector.tensor_tensor(mT[:, c, :], sg[c % 2], up_ps(c), ALU.mult).then_inc(m_made, 1)
            dve.wait_ge(xr_made, 1)
            for b in range(0, B, 2):
                dve.wait_ge(down_done, b // 2 + 1)
                nc.vector.tensor_tensor(x1[:, b:b + 2, :].rearrange("p b d -> p (b d)"),
                                        xr[:, b:b + 2, :].rearrange("p b d -> p (b d)"), ps[:, b * D:(b + 2) * D], ALU.add)

        @block.scalar
        def _(act):
            for b in range(B):
                act.wait_ge(xa_made, b + 1)
                if b:
                    act.wait_ge(ms_made, b)
                nc.scalar.activation(sqr, xa[:, b, :], ACT.Square, accum_out=ms[:, b:b + 1]).then_inc(ms_made, 1)
            act.wait_ge(x_in, 48)
            act.wait_ge(h2T_done, 1)
            for k in range(KD):
                nc.scalar.activation(h2T[:, k, :], hps[:, k, :], ACT.Copy, scale=ln2[:, k:k + 1]).then_inc(h2T_made, 1)
            for c in range(NI):
                act.wait_ge(gate_done, c + 1)
                if c >= 2:
                    act.wait_ge(m_made, c - 1)
                nc.scalar.activation(sg[c % 2], gate_ps(c), ACT.Silu).then_inc(sg_made, 1)

        @block.gpsimd
        def _(pool):
            pool.wait_ge(ms_made, B)
            nc.gpsimd.tensor_scalar(tmp, ms, 1.0 / D, 1e-6, ALU.mult, ALU.add).then_inc(pool_step, 1)
            pool.wait_ge(pool_step, 1)
            nc.gpsimd.tensor_tensor(rms, tmp, fixed["mhalf"].broadcast_to([P, B]), ALU.pow).then_inc(rms_made, 1)
            pool.wait_ge(x_in, 48)
            nc.gpsimd.tensor_tensor(xr, xr, xa, ALU.add).then_inc(xr_made, 1)


def layernorm_stats(nc, dve, pool_like, x, stats, mv, done, step):
    for b in range(B):
        nc.vector.bn_stats(stats[:, b, :], x[:, b, :]).then_inc(step, 1)
    for b in range(B):
        dve.wait_ge(step, b + 1)
        nc.vector.bn_aggr(mv[:, b, :], stats[:, b, :]).then_inc(done, 1)


def expert_loads(sp, a, ring, g, slot, arrived):
    wgu, wd = ring["wgu"][slot], ring["wd"][slot]
    for j, name in enumerate(("e_gate", "e_up")):
        for k in range(KD):
            sp.dma_start(wgu[:, :, k, j * I2:(j + 1) * I2],
                         a[name].rearrange("(g e) (p k) n -> g k p e n", e=GRP, k=KD)[g, k]).then_inc(arrived, 16)
    sp.dma_start(wd[0:IH], a["e_down"].rearrange("(g e) (p c) n -> g p e (c n)", e=GRP, c=2)[g]
                 .rearrange("p e (c n) -> p e c n", c=2)).then_inc(arrived, 16)


LOADS = 5 * 16


def build_cross(nc, a, fixed, room, ps, ring, ring_in):
    consts, x1, mhalf = fixed["consts"], fixed["x1"], fixed["mhalf"]
    ident = consts[:, CONST["ident"][0]:CONST["ident"][1]]
    evenodd = consts[:, CONST["evenodd"][0]:CONST["evenodd"][1]]
    NJ = XH // 2
    yq = room.take(B, D)
    stats, mv = room.take(B, 6), room.take(B, 2)
    r1, r2, r3 = room.take(B), room.take(B), room.take(B)
    gam = room.take(1)
    yb = [room.take(D) for _ in range(2)]
    cb = [room.take(D) for _ in range(2)]
    cm = [room.take(2, D) for _ in range(2)]
    cT = [room.take(2, XH, XD + 1) for _ in range(2)]
    pr = [room.take(2, D) for _ in range(2)]
    prT = [room.take(2, 2, P) for _ in range(2)]
    nmax = room.take(2, 2)
    ret = room.take(2, XH, XD)
    rec = room.take(2, XH, 1)

    def bank(i):
        return ps[:, i * HALF:(i + 1) * HALF]

    res_ps = bank(4)[:, 0:2 * XH * (XD + 1)].rearrange("p (q h c) -> p q h c", q=2, h=XH)
    cT_ps = bank(5)[:, 0:2 * P].rearrange("p (l h c) -> p l h c", l=2, h=XH)
    rT_ps = bank(6)[:, 0:D]
    NU = NJ * 2

    with ExitStack() as ctx:
        def sem(name):
            return ctx.enter_context(nc.semaphore(name))

        stat_step, stat_made, r_step, r_made, yq_made = sem("xstat_step"), sem("xstat_made"), sem("xr_step"), sem("xr_made"), sem("yq_made")
        gam_in, cb_in, yb_made, cm_made = sem("gam_in"), [sem(f"ctx_in{i}") for i in range(2)], sem("yb_made"), sem("cm_made")
        cT_done, cT_made, ones_made = sem("cT_done"), sem("cT_made"), sem("cT_ones_made")
        s_done, max_made, exp_made, pT_done, pT_made, res_done = sem("score_done"), sem("max_made"), sem("xexp_made"), sem("pT_done"), sem("pT_made"), sem("res_done")
        rec_made, ret_made, rT_done, x2_made = sem("rec_made"), sem("ret_made"), sem("rT_done"), sem("x2_made")
        block = ctx.enter_context(nc.Block())

        @block.sync
        def _(sp):
            sp.dma_start(gam, a["gamma"].partition_broadcast(P)).then_inc(gam_in, 16)

            def load(b, par):
                if not (isinstance(b, int) and b < 2):
                    sp.wait_ge(cm_made, 2 * b - 2)
                    sp.nop(nofuse=True)
                    sp.wait_ge(cT_done, b - 1)
                    sp.nop(nofuse=True)
                sp.dma_start(cb[par], a["ctx"][b]).then_inc(cb_in[par], 16)
            load(0, 0)
            load(1, 1)
            for g in range(RING):
                expert_loads(sp, a, ring, g, g, ring_in[g])
            with sp.Fori(1, B // 2) as i:
                load(i * 2, 0)
                load(i * 2 + 1, 1)

        @block.gpsimd
        def _(pool):
            for par in range(2):
                nc.gpsimd.memset(cT[par][:, :, :, XD:XD + 1], 1.0).then_inc(ones_made, 1)
            pool.wait_ge(stat_made, B)
            nc.gpsimd.tensor_scalar(r1, mv[:, :, 1], 1e-5, None, ALU.add).then_inc(r_step, 1)
            pool.wait_ge(r_step, 1)
            nc.gpsimd.tensor_tensor(r2, r1, mhalf.broadcast_to([P, B]), ALU.pow).then_inc(r_step, 1)
            pool.wait_ge(r_step, 2)
            nc.gpsimd.tensor_scalar(r3, r2, XD ** -0.5, None, ALU.mult).then_inc(r_made, 1)

            def body(b, par):
                if not (isinstance(b, int) and b < 2):
                    pool.wait_ge(s_done, NU * b - NU)
                pool.wait_ge(yq_made, B)
                pool.nop(nofuse=True)
                nc.gpsimd.tensor_copy(yb[par], yq[:, b, :]).then_inc(yb_made, 1)
                pool.wait_ge(cb_in[par], 16 * turn(b, 2))
                pool.nop(nofuse=True)
                for o in range(2):
                    nc.gpsimd.tensor_scalar(cm[par][:, o, :], cb[par], evenodd[:, o:o + 1], None, ALU.mult).then_inc(cm_made, 1)
            body(0, 0)
            body(1, 1)
            with pool.Fori(1, B // 2) as i:
                body(i * 2, 0)
                body(i * 2 + 1, 1)

        @block.tensor
        def _(pe):
            def scores(b, par, un):
                j, q = un // 2, un % 2
                need(pe, exp_made, NU * b + un - 1)
                s = slice(j * QB, (j + 1) * QB)
                nc.tensor.matmul(bank(un % 2), yb[par][s, q * P:(q + 1) * P], cm[par][s].rearrange("p o l -> p (o l)"),
                                 start=True, stop=True).then_inc(s_done, 1)

            def ctx_T(b, par):
                pe.wait_ge(cb_in[par], 16 * turn(b, 2))
                need(pe, cT_made, b)
                for l in range(2):
                    last = nc.tensor.transpose(bank(5)[:, l * P:(l + 1) * P], cb[par][:, l * P:(l + 1) * P], ident)
                last.then_inc(cT_done, 1)

            def transposes(b, un):
                pe.wait_ge(exp_made, NU * b + un + 1)
                need(pe, pT_made, NU * b + un - 1)
                for o in range(2):
                    for l in range(2):
                        last = nc.tensor.transpose(bank(2 + un % 2)[:, (2 * o + l) * P:(2 * o + l + 1) * P],
                                                   pr[un % 2][:, o, l * P:(l + 1) * P], ident)
                last.then_inc(pT_done, 1)

            def values(b, par, un):
                j, q = un // 2, un % 2
                pe.wait_ge(pT_made, NU * b + un + 1)
                if un == 0:
                    pe.wait_ge(cT_made, b + 1)
                    need(pe, ret_made, b)
                for o in range(2):
                    for l in range(2):
                        last = nc.tensor.matmul(res_ps[:, q, 2 * j + o, :], prT[un % 2][:, o, l, :], cT[par][:, l, 2 * j + o, :],
                                                start=(l == 0), stop=(l == 1))
                last.then_inc(res_done, 1)

            def body(b, par):
                ctx_T(b, par)
                pe.wait_ge(yb_made, b + 1)
                pe.wait_ge(cm_made, 2 * b + 2)
                scores(b, par, 0)
                scores(b, par, 1)
                for un in range(NU):
                    transposes(b, un)
                    if un + 2 < NU:
                        scores(b, par, un + 2)
                    if un:
                        values(b, par, un - 1)
                values(b, par, NU - 1)
                pe.wait_ge(ret_made, b + 1)
                need(pe, x2_made, b)
                for q in range(2):
                    last = nc.tensor.transpose(rT_ps[:, q * P:(q + 1) * P], ret[:, q].rearrange("p h c -> p (h c)"), ident)
                last.then_inc(rT_done, 1)

            body(0, 0)
            body(1, 1)
            with pe.Fori(1, B // 2) as i:
                body(i * 2, 0)
                body(i * 2 + 1, 1)

        @block.vector
        def _(dve):
            layernorm_stats(nc, dve, None, x1, stats, mv, stat_made, stat_step)
            dve.wait_ge(r_made, 1)
            dve.wait_ge(stat_made, B)
            for b in range(B):
                nc.vector.tensor_scalar(yq[:, b, :], x1[:, b, :], mv[:, b, 0:1], r3[:, b:b + 1],
                                        ALU.subtract, ALU.mult).then_inc(yq_made, 1)
            dve.wait_ge(gam_in, 16)

            def maxima(b, un):
                dve.wait_ge(s_done, NU * b + un + 1)
                need(dve, exp_made, NU * b + un - 1)
                nc.vector.tensor_reduce(nmax[:, un % 2, :], bank(un % 2).rearrange("p (o l) -> p o l", o=2), AX_X, ALU.max,
                                        negate=True).then_inc(max_made, 1)

            def copy_T(b, un):
                dve.wait_ge(pT_done, NU * b + un + 1)
                need(dve, res_done, NU * b + un - 1)
                nc.vector.tensor_copy(prT[un % 2].rearrange("p o l q -> p (o l q)"), bank(2 + un % 2)).then_inc(pT_made, 1)

            def body(b, par):
                dve.wait_ge(cT_done, b + 1)
                if not (isinstance(b, int) and b < 2):
                    dve.wait_ge(res_done, NU * b - NU)
                dve.wait_ge(ones_made, 2)
                nc.vector.tensor_copy(cT[par][:, :, :, 0:XD], cT_ps).then_inc(cT_made, 1)
                maxima(b, 0)
                maxima(b, 1)
                for un in range(NU):
                    copy_T(b, un)
                    if un + 2 < NU:
                        maxima(b, un + 2)
                dve.wait_ge(res_done, NU * b + NU)
                need(dve, rT_done, b)
                nc.vector.reciprocal(rec, res_ps[:, :, :, XD:XD + 1]).then_inc(rec_made, 1)
                dve.wait_ge(rec_made, b + 1)
                nc.vector.tensor_tensor(ret, res_ps[:, :, :, 0:XD], rec.broadcast_to([P, 2, XH, XD]), ALU.mult).then_inc(ret_made, 1)
                dve.wait_ge(rT_done, b + 1)
                nc.vector.scalar_tensor_tensor(x1[:, b, :], rT_ps, gam, x1[:, b, :], ALU.mult, ALU.add).then_inc(x2_made, 1)

            body(0, 0)
            body(1, 1)
            with dve.Fori(1, B // 2) as i:
                body(i * 2, 0)
                body(i * 2 + 1, 1)

        @block.scalar
        def _(act):
            def body(b, par):
                for un in range(NU):
                    act.wait_ge(max_made, NU * b + un + 1)
                    need(act, pT_done, NU * b + un - 1)
                    for o in range(2):
                        last = nc.scalar.activation(pr[un % 2][:, o, :], bank(un % 2)[:, o * D:(o + 1) * D], ACT.Exp,
                                                    bias=nmax[:, un % 2, o:o + 1])
                    last.then_inc(exp_made, 1)
            body(0, 0)
            body(1, 1)
            with act.Fori(1, B // 2) as i:
                body(i * 2, 0)
                body(i * 2 + 1, 1)


def build_route(nc, a, fixed, room, ps, scratch):
    consts, x2, mhalf = fixed["consts"], fixed["x1"], fixed["mhalf"]

    def const(name):
        return consts[:, CONST[name][0]:CONST[name][1]]

    ident = const("ident")
    xf = room.take(B, D)
    xfT = fixed["xfT"]
    wr = room.take(D)
    wrT = room.take(KD, E)
    stats, mv = room.take(B, 6), room.take(B, 2)
    r1, r2 = room.take(B), room.take(B)
    lg = room.take(B, E)
    top = room.take(B, 8)
    idx = room.take(B, 8).bitcast(U32)
    idf = room.take(B, K4)
    ex = room.take(B, K4)
    sm = room.take(B, 1)
    oh = [room.take(B, E) for _ in range(K4)]
    m2 = [room.take(B, E) for _ in range(2)]
    mb = room.take(B, E // 2).bitcast(BF16)
    onesb = room.take(P // 2).bitcast(BF16)
    beforeb = room.take(P // 2).bitcast(BF16)
    tmp = [room.take(B, E) for _ in range(2)]
    pos = room.take(K4, B)
    val, sl, sf = room.take(K4, B), room.take(K4, B), room.take(K4, B)
    wtok, slots = fixed["wtok"], fixed["slots"]

    with ExitStack() as ctx:
        def sem(name):
            return ctx.enter_context(nc.semaphore(name))

        wr_in, stat_step, stat_made, r_step, xf_made = sem("wr_in"), sem("rstat_step"), sem("rstat_made"), sem("rr_step"), sem("xf_made")
        wrT_done, wrT_made, xfT_done, xfT_made, lg_done = sem("wrT_done"), sem("wrT_made"), sem("xfT_done"), sem("xfT_made"), sem("lg_done")
        step, ex_in, ex_made, m_made, pos_done, slots_made = sem("route_step"), sem("ex_in"), sem("rexp_made"), sem("choice_made"), sem("pos_done"), sem("slots_made")
        rows_out, cvt = sem("rows_out"), sem("bf16_made")
        block = ctx.enter_context(nc.Block())
        hps = ps[:, 0:2 * TOK].rearrange("p (k n) -> p k n", k=KD)
        wps = ps[:, 4 * HALF:4 * HALF + KD * E].rearrange("p (k e) -> p k e", k=KD)
        lps = ps[:, 5 * HALF:6 * HALF].rearrange("p (b e) -> p b e", b=B)
        pps = ps[:, 6 * HALF:7 * HALF].rearrange("p (b e) -> p b e", b=B)

        @block.sync
        def _(sp):
            sp.dma_start(wr[0:E], a["w_router"]).then_inc(wr_in, 16)

        @block.tensor
        def _(pe):
            pe.wait_ge(wr_in, 16)
            for k in range(KD):
                last = nc.tensor.transpose(wps[:, k, :], wr[0:E, k * P:(k + 1) * P], ident[0:E, 0:E])
            last.then_inc(wrT_done, 1)
            for b in range(B):
                pe.wait_ge(xf_made, b + 1)
                for k in range(KD):
                    last = nc.tensor.transpose(hps[:, k, b * P:(b + 1) * P], xf[:, b, k * P:(k + 1) * P], ident)
            last.then_inc(xfT_done, 1)
            pe.wait_ge(wrT_made, 1)
            pe.wait_ge(xfT_made, KD)
            for b in range(B):
                for k in range(KD):
                    last = nc.tensor.matmul(lps[:, b, :], xfT[:, k, b * P:(b + 1) * P], wrT[:, k, :],
                                            start=(k == 0), stop=(k == KD - 1))
            last.then_inc(lg_done, 1)
            pe.wait_ge(m_made, 1)
            pe.wait_ge(cvt, 2)
            for b in range(B):
                for b2 in range(b + 1):
                    last = nc.tensor.matmul(pps[:, b, :], beforeb if b2 == b else onesb, mb[:, b2, :],
                                            start=(b2 == 0), stop=(b2 == b))
            last.then_inc(pos_done, 1)

        @block.scalar
        def _(act):
            nc.scalar.activation(onesb, const("ones"), ACT.Copy).then_inc(cvt, 1)
            nc.scalar.activation(beforeb, const("before"), ACT.Copy).then_inc(cvt, 1)
            act.wait_ge(wrT_done, 1)
            nc.scalar.activation(wrT, wps, ACT.Copy).then_inc(wrT_made, 1)
            act.wait_ge(xfT_done, 1)
            for k in range(KD):
                nc.scalar.activation(xfT[:, k, :], hps[:, k, :], ACT.Copy).then_inc(xfT_made, 1)
            act.wait_ge(ex_in, 1)
            nc.scalar.activation(ex, ex, ACT.Exp).then_inc(ex_made, 1)

        @block.vector
        def _(dve):
            n = [0]

            def then(ins):
                n[0] += 1
                ins.then_inc(step, 1)
                dve.wait_ge(step, n[0])

            layernorm_stats(nc, dve, None, x2, stats, mv, stat_made, stat_step)
            dve.wait_ge(r_step, 2)
            for b in range(B):
                nc.vector.tensor_scalar(xf[:, b, :], x2[:, b, :], mv[:, b, 0:1], r2[:, b:b + 1],
                                        ALU.subtract, ALU.mult).then_inc(xf_made, 1)
            dve.wait_ge(lg_done, 1)
            then(nc.vector.tensor_copy(lg, lps))
            for b in range(B):
                last = nc.vector.max(top[:, b, :], lg[:, b, :])
            then(last)
            for b in range(B):
                last = nc.vector.max_index(idx[:, b, :], top[:, b, :], lg[:, b, :])
            then(last)
            nc.vector.tensor_tensor(ex, top[:, :, 0:K4], top[:, :, 0:1].broadcast_to([P, B, K4]), ALU.subtract).then_inc(ex_in, 1)
            then(nc.vector.tensor_copy(idf, idx[:, :, 0:K4]))
            for j in range(K4):
                last = nc.vector.tensor_tensor(oh[j], const("iota").unsqueeze(1).broadcast_to([P, B, E]),
                                               idf[:, :, j:j + 1].broadcast_to([P, B, E]), ALU.is_equal)
            then(last)
            nc.vector.tensor_tensor(m2[0], oh[0], oh[1], ALU.add)
            then(nc.vector.tensor_tensor(m2[1], oh[2], oh[3], ALU.add))
            nc.vector.tensor_tensor(mb, m2[0], m2[1], ALU.add).then_inc(m_made, 1)
            dve.wait_ge(ex_made, 1)
            then(nc.vector.tensor_reduce(sm.rearrange("p b o -> p (b o)"), ex, AX_X, ALU.add))
            then(nc.vector.reciprocal(sm, sm))
            nc.vector.tensor_tensor(wtok, ex, sm.broadcast_to([P, B, K4]), ALU.mult)
            dve.wait_ge(pos_done, 1)
            for j in range(K4):
                then(nc.vector.tensor_tensor(tmp[j % 2], oh[j], pps, ALU.mult))
                then(nc.vector.tensor_reduce(pos[:, j, :], tmp[j % 2], AX_X, ALU.add))
            nc.vector.tensor_scalar(val, pos, float(C), None, ALU.is_lt)
            then(nc.vector.scalar_tensor_tensor(sl, idf.rearrange("p b j -> p j b"), float(C), pos, ALU.mult, ALU.add))
            then(nc.vector.scalar_tensor_tensor(sf, sl, float(-SLOTS), val, ALU.add, ALU.mult))
            nc.vector.tensor_scalar(slots, sf, float(SLOTS), None, ALU.add).then_inc(slots_made, 1)

        @block.gpsimd
        def _(pool):
            pool.wait_ge(stat_made, B)
            nc.gpsimd.tensor_scalar(r1, mv[:, :, 1], 1e-5, None, ALU.add).then_inc(r_step, 1)
            pool.wait_ge(r_step, 1)
            nc.gpsimd.tensor_tensor(r2, r1, mhalf.broadcast_to([P, B]), ALU.pow).then_inc(r_step, 1)
            pool.wait_ge(slots_made, 1)
            for b in range(B):
                for j in range(K4):
                    nc.gpsimd.indirect_dma_start(
                        scratch["rows"], bass.IndirectOffsetOnAxis(slots[:, j, b:b + 1], 0), xf[:, b, :], None,
                        bounds_check=SLOTS - 1, oob_is_err=False).then_inc(rows_out, 16)
            pool.wait_ge(rows_out, 16 * B * K4)


def build_experts(nc, a, fixed, room, ps, scratch, ring, ring_in, out):
    consts, x2, xfT, wtok, slots = fixed["consts"], fixed["x1"], fixed["xfT"], fixed["wtok"], fixed["slots"]
    ident = consts[:, CONST["ident"][0]:CONST["ident"][1]]
    wsg = room.take(KD, I2)
    wsu = room.take(KD, I2)
    wsd = room.take(2, D)
    xg = [room.take(D) for _ in range(2)]
    xT = [room.take(KD, P) for _ in range(2)]
    sg = [room.take(I2) for _ in range(2)]
    gu = [room.take(I2) for _ in range(2)]
    guT = [room.take(2, P) for _ in range(2)]
    y = [room.take(D) for _ in range(2)]
    ssg = room.take(TOK)
    smT = room.take(2, TOK)
    yg = [room.take(K4, D) for _ in range(4)]
    acc = [room.take(B, D) for _ in range(2)]

    def bank(i):
        return ps[:, i * HALF:(i + 1) * HALF]

    with ExitStack() as ctx:
        def sem(name):
            return ctx.enter_context(nc.semaphore(name))

        ws_in = sem("ws_in")
        xg_in = [sem(f"xg_in{i}") for i in range(2)]
        xT_done, xT_made, gu_done, sg_made, gu_made = sem("xT_done"), sem("xT_made"), sem("gu_done"), sem("esg_made"), sem("gu_made")
        guT_done, guT_made, y_done, y_made = sem("guT_done"), sem("guT_made"), sem("y_done"), sem("y_made")
        y_out = [sem(f"y_out{i}") for i in range(2)]
        sh_gate_done, sh_up_done, sh_sg_made, sh_m_made, sh_done, base_made = (
            sem("sh_gate_done"), sem("sh_up_done"), sem("sh_sg_made"), sem("sh_m_made"), sem("sh_done"), sem("base_made"))
        yg_in = [sem(f"yg_in{i}") for i in range(4)]
        acc_step, out_done = sem("acc_step"), sem("out_done")
        block = ctx.enter_context(nc.Block())

        def groups(eng, body):
            body(-1, RING - 1, False, True)
            for s in range(RING):
                body(s, s, True, True)
            with eng.Fori(1, (NG - RING) // RING) as i:
                for s in range(RING):
                    body(i * RING + s, s, True, True)
            for s in range(RING):
                body(NG - RING + s, s, True, s < RING - 1)

        @block.sync
        def _(sp):
            for dst, name in ((wsg, "sh_gate"), (wsu, "sh_up")):
                sp.dma_start(dst, a[name].rearrange("(k p) n -> p k n", p=P)).then_inc(ws_in, 16)
            sp.dma_start(wsd[0:IH], a["sh_down"].rearrange("(c p) n -> p c n", p=IH)).then_inc(ws_in, 16)

            def rows(g, par):
                if not (isinstance(g, int) and g < 2):
                    sp.wait_ge(xT_done, g - 1)
                    sp.nop(nofuse=True)
                sp.dma_start(xg[par], scratch["rows"].rearrange("(g p) d -> g p d", p=P)[g]).then_inc(xg_in[par], 16)
            rows(0, 0)
            rows(1, 1)
            with sp.Fori(0, (NG - RING) // RING) as i:
                for s in range(RING):
                    rows(i * RING + (s + 2), s % 2)
                    sp.wait_ge(y_done, i * RING + (s + 1))
                    sp.nop(nofuse=True)
                    expert_loads(sp, a, ring, i * RING + (s + RING), s, ring_in[s])
            rows(NG - 2, 0)
            rows(NG - 1, 1)

        @block.tensor
        def _(pe):
            def body(g, s, back, front):
                f, fs = g + 1, (s + 1) % RING
                par, fpar = s % 2, (s + 1) % 2
                if front:
                    pe.wait_ge(xg_in[fpar], 16 * turn(f, 2))
                    need(pe, xT_made, f - 1)
                    for k in range(KD):
                        last = nc.tensor.transpose(bank(fpar)[:, k * P:(k + 1) * P],
                                                   xg[fpar].rearrange("p (c k) -> p k c", k=KD)[:, k, :], ident)
                    last.then_inc(xT_done, 1)
                if back:
                    pe.wait_ge(gu_made, g + 1)
                    for c in range(2):
                        last = nc.tensor.transpose(bank(4 + par)[0:IH, c * P:(c + 1) * P],
                                                   gu[par].rearrange("p (i c) -> p c i", c=2)[:, c, :], ident)
                    last.then_inc(guT_done, 1)
                if front:
                    pe.wait_ge(xT_made, f + 1)
                    pe.wait_ge(ring_in[fs], LOADS * turn(f, RING))
                    need(pe, gu_made, f - 1)
                    for e in range(GRP):
                        for k in range(KD):
                            last = nc.tensor.matmul(bank(2 + fpar)[e * C:(e + 1) * C, 0:2 * I2], xT[fpar][:, k, e * C:(e + 1) * C],
                                                    ring["wgu"][fs][:, e, k, :], start=(k == 0), stop=(k == KD - 1))
                    last.then_inc(gu_done, 1)
                if back:
                    pe.wait_ge(guT_made, g + 1)
                    need(pe, y_made, g)
                    for e in range(GRP):
                        for c in range(2):
                            last = nc.tensor.matmul(bank(6 + par)[e * C:(e + 1) * C, 0:D], guT[par][0:IH, c, e * C:(e + 1) * C],
                                                    ring["wd"][s][0:IH, e, c, :], start=(c == 0), stop=(c == 1))
                    last.then_inc(y_done, 1)

            pe.wait_ge(ws_in, 48)
            for c in range(2):
                if c:
                    pe.wait_ge(sh_m_made, 1)
                for w, dst, done in ((wsg, ps[:, 0:TOK], sh_gate_done), (wsu, ps[:, TOK:2 * TOK], sh_up_done)):
                    for n in range(2):
                        for k in range(KD):
                            last = nc.tensor.matmul(dst[0:IH, n * HALF:(n + 1) * HALF], w[:, k, c * IH:(c + 1) * IH],
                                                    xfT[:, k, n * HALF:(n + 1) * HALF], start=(k == 0), stop=(k == KD - 1))
                    last.then_inc(done, 1)
            pe.wait_ge(sh_m_made, 2)
            for b in range(B):
                for c in range(2):
                    last = nc.tensor.matmul(ps[:, 2 * TOK + b * D:2 * TOK + (b + 1) * D], smT[0:IH, c, b * P:(b + 1) * P],
                                            wsd[0:IH, c, :], start=(c == 0), stop=(c == 1))
            last.then_inc(sh_done, 1)
            pe.wait_ge(base_made, 1)
            groups(pe, body)

        @block.scalar
        def _(act):
            for c in range(2):
                act.wait_ge(sh_gate_done, c + 1)
                if c:
                    act.wait_ge(sh_m_made, 1)
                nc.scalar.activation(ssg[0:IH], ps[0:IH, 0:TOK], ACT.Silu).then_inc(sh_sg_made, 1)

            def body(g, s, back, front):
                f = g + 1
                par, fpar = s % 2, (s + 1) % 2
                if front:
                    act.wait_ge(gu_done, f + 1)
                    need(act, gu_made, f - 1)
                    nc.scalar.activation(sg[fpar], bank(2 + fpar)[:, 0:I2], ACT.Silu).then_inc(sg_made, 1)
                if back:
                    act.wait_ge(y_done, g + 1)
                    if not (isinstance(g, int) and g < 2):
                        act.wait_ge(y_out[par], 16 * turn(g, 2) - 16)
                    nc.scalar.activation(y[par], bank(6 + par)[:, 0:D], ACT.Copy).then_inc(y_made, 1)
                    act.wait_ge(y_made, g + 1)
                    act.dma_start(scratch["results"][0:SLOTS].rearrange("(g p) d -> g p d", p=P)[g], y[par]).then_inc(y_out[par], 16)

            groups(act, body)
            for b in range(B):
                act.wait_ge(acc_step, K4 * (b + 1))
                act.dma_start(out[b], acc[(K4 - 1) % 2][:, b, :]).then_inc(out_done, 16)
            act.wait_ge(out_done, 16 * B)

        @block.vector
        def _(dve):
            for c in range(2):
                dve.wait_ge(sh_sg_made, c + 1)
                dve.wait_ge(sh_up_done, c + 1)
                nc.vector.tensor_tensor(smT[0:IH, c, :], ssg[0:IH], ps[0:IH, TOK:2 * TOK], ALU.mult).then_inc(sh_m_made, 1)
            dve.wait_ge(sh_done, 1)
            nc.vector.tensor_tensor(acc[1].rearrange("p b d -> p (b d)"), x2.rearrange("p b d -> p (b d)"),
                                    ps[:, 2 * TOK:4 * TOK], ALU.add).then_inc(base_made, 1)

            def body(g, s, back, front):
                f = g + 1
                par, fpar = s % 2, (s + 1) % 2
                if front:
                    dve.wait_ge(xT_done, f + 1)
                    need(dve, gu_done, f - 1)
                    nc.vector.tensor_copy(xT[fpar].rearrange("p k c -> p (k c)"), bank(fpar)[:, 0:D]).then_inc(xT_made, 1)
                if back:
                    dve.wait_ge(guT_done, g + 1)
                    nc.vector.tensor_copy(guT[par][0:IH].rearrange("p c n -> p (c n)"), bank(4 + par)[0:IH, 0:2 * P]).then_inc(guT_made, 1)
                if front:
                    dve.wait_ge(sg_made, f + 1)
                    need(dve, guT_done, f - 1)
                    nc.vector.tensor_tensor(gu[fpar], sg[fpar], bank(2 + fpar)[:, I2:2 * I2], ALU.mult).then_inc(gu_made, 1)

            groups(dve, body)
            dve.wait_ge(base_made, 1)
            for b in range(B):
                dve.wait_ge(yg_in[b % 4], 16 * K4 * (b // 4 + 1))
                for j in range(K4):
                    if j:
                        dve.wait_ge(acc_step, K4 * b + j)
                    nc.vector.scalar_tensor_tensor(acc[j % 2][:, b, :],
                                                   yg[b % 4][:, j, :], wtok[:, b, j:j + 1], acc[(j + 1) % 2][:, b, :],
                                                   ALU.mult, ALU.add).then_inc(acc_step, 1)

        @block.gpsimd
        def _(pool):
            for par in range(2):
                pool.wait_ge(y_out[par], 16 * (NG // 2))
            for b in range(B):
                if b >= 4:
                    pool.wait_ge(acc_step, K4 * (b - 3))
                for j in range(K4):
                    nc.gpsimd.indirect_dma_start(yg[b % 4][:, j, :], None, scratch["results"],
                                                 bass.IndirectOffsetOnAxis(slots[:, j, b:b + 1], 0),
                                                 bounds_check=SLOTS, oob_is_err=True).then_inc(yg_in[b % 4], 16)


def turn(g, n):
    return g // n + 1


NAMES = {
    "x": "x", "ctx": "ctx_2048", "wq": "L0_attn_wq", "wk": "L0_attn_wk", "wv": "L0_attn_wv", "conv_q": "L0_attn_conv_q",
    "conv_k": "L0_attn_conv_k", "conv_v": "L0_attn_conv_v", "wfa": "L0_attn_wfa", "wfb": "L0_attn_wfb", "wb": "L0_attn_wb",
    "wga": "L0_attn_wga", "wgb": "L0_attn_wgb", "a_log": "L0_attn_a_log", "dt_bias": "L0_attn_dt_bias",
    "o_norm_w": "L0_attn_o_norm_w", "wo": "L0_attn_wo", "ln1_w": "L0_attn_ln1_w", "ln2_w": "L0_attn_ln2_w",
    "w_gate": "L0_attn_w_gate", "w_up": "L0_attn_w_up", "w_down": "L0_attn_w_down", "gamma": "L0_xattn_gamma",
    "w_router": "L0_ffn_w_router", "e_gate": "L0_ffn_w_gate", "e_up": "L0_ffn_w_up", "e_down": "L0_ffn_w_down",
    "sh_gate": "L0_ffn_w_sh_gate", "sh_up": "L0_ffn_w_sh_up", "sh_down": "L0_ffn_w_sh_down",
}
ARENA = 53200


def decoder_kernel(nc, a, out, scratch):
    with ExitStack() as ctx:
        arena = ctx.enter_context(nc.sbuf_tensor("arena", [P, ARENA], F32))
        psum = ctx.enter_context(nc.psum_tensor("psum", [P, 8 * HALF], F32))
        ring_in = [ctx.enter_context(nc.semaphore(f"ring_in{i}")) for i in range(RING)]
        zero_out = ctx.enter_context(nc.semaphore("zero_out"))
        ps = psum[:, :]
        base = Room(arena, 0)
        fixed = {"consts": base.take(NCONST), "mhalf": base.take(1), "onw": base.take(1), "x0": base.take(B, D)}
        low = base.at
        fixed["hT"] = base.take(KD, TOK)
        fixed["lowg"] = base.take(TOK)
        fixed["heads"] = base.take(H, HT)
        after_prepare = base.at
        prep = Room(arena, after_prepare)
        clear_semaphores(nc, build_prepare(nc, a, fixed, prep, ps))
        fixed["o_all"] = base.take(H, TOK)
        clear_semaphores(nc, build_delta(nc, a, fixed, base, ps))

        fixed["x1"] = Room(arena, low).take(B, D)
        build_mlp(nc, a, fixed, Room(arena, after_prepare + H * TOK), ps)

        rest = Room(arena, low + B * D)
        ring = {"wgu": [rest.take(GRP, KD, 2 * I2) for _ in range(RING)], "wd": [rest.take(GRP, 2, D) for _ in range(RING)]}
        fixed["xfT"] = rest.take(KD, TOK)
        fixed["wtok"] = rest.take(B, K4)
        fixed["slots"] = rest.take(K4, B).bitcast(U32)
        build_cross(nc, a, fixed, Room(arena, rest.at), ps, ring, ring_in)
        build_zero(nc, Room(arena, rest.at), scratch, zero_out)
        build_route(nc, a, fixed, Room(arena, rest.at), ps, scratch)
        build_experts(nc, a, fixed, Room(arena, rest.at), ps, scratch, ring, ring_in, out)


def build_zero(nc, room, scratch, zero_out):
    z = room.take(D)
    with ExitStack() as ctx:
        z_made = ctx.enter_context(nc.semaphore("zeros_made"))
        block = ctx.enter_context(nc.Block())

        @block.gpsimd
        def _(pool):
            nc.gpsimd.memset(z, 0.0).then_inc(z_made, 1)

        @block.sync
        def _(sp):
            sp.wait_ge(z_made, 1)
            sp.dma_start(scratch["rows"].rearrange("(g p) d -> p g d", p=P),
                         z.unsqueeze(1).broadcast_to([P, SLOTS // P, D])).then_inc(zero_out, 16)
            sp.dma_start(scratch["results"][SLOTS:SLOTS + 1], z[0:1]).then_inc(zero_out, 16)
            sp.wait_ge(zero_out, 32)


def kernel(**inputs):
    import numpy as np
    import concourse.bacc as bacc
    from concourse.bass_utils import run_bass_kernel_spmd

    nc = bacc.Bacc("TRN2", target_bir_lowering=False, num_devices=1)
    arrays, a = {}, {}
    for name, full in NAMES.items():
        v = np.ascontiguousarray(inputs[full])
        if v.ndim == 0:
            v = v.reshape(1)
        arrays["in_" + name] = v
    arrays["in_consts"] = constant_table(np)
    for key, v in arrays.items():
        a[key[3:]] = nc.dram_tensor(key, v.shape, mybir.dt.from_np(v.dtype), kind="ExternalInput").ap()
    out = nc.dram_tensor("out", (B, P, D), F32, kind="ExternalOutput").ap()
    scratch = {"rows": nc.dram_tensor("rows", (SLOTS, D), F32, kind="Internal").ap(),
               "results": nc.dram_tensor("results", (SLOTS + 1, D), F32, kind="Internal").ap()}
    decoder_kernel(nc, a, out, scratch)
    got = run_bass_kernel_spmd(nc, [arrays], core_ids=[0])
    return got.results[0]["out"]
```

```python
from contextlib import ExitStack

import concourse.bass as bass
from concourse import mybir

ACT = mybir.ActivationFunctionType
ALU = mybir.AluOpType
F32 = mybir.dt.float32
BF16 = mybir.dt.bfloat16
F16 = mybir.dt.float16
U32 = mybir.dt.uint32
AX_X = mybir.AxisListType.X

P = 128
B = 8
D = 256
KD = D // P
TOK = B * P
H = 16
HALF = TOK // 2
I1 = 1024
NI = I1 // P
XH = 8
XD = P // XH
E = 64
K4 = 4
C = 32
SLOTS = E * C
I2 = 192
IH = I2 // 2
GRP = P // C
NG = E // GRP
RING = 4
QB = 32
NQ = P // QB
LOGQ = 5

CONST = {}
_at = 0
for _name, _n in (("ident", P), ("incl", P), ("strict", P), ("ylevel", (LOGQ - 1) * P), ("identc", QB), ("level0", QB),
                  ("diag", P), ("ones", P), ("iota", E), ("before", P), ("headmask", XH)):
    CONST[_name] = (_at, _at + _n)
    _at += _n
NCONST = _at

HT_CONV, HT_G, HT_SB, HT = 0, 12, 12 + B, 12 + 2 * B


def constant_table(np):
    r = np.arange(P)[:, None]
    c = np.arange(P)[None, :]
    j = np.arange(QB)[None, :]
    t = np.zeros((P, NCONST), np.float32)

    def put(name, v):
        a, b = CONST[name]
        t[:, a:b] = v

    put("ident", r == c)
    put("incl", r <= c)
    put("strict", r > c)
    put("before", r < c)
    put("ylevel", np.concatenate([((r >> (k + 1)) == (c >> (k + 1))) & ((r >> k) % 2 == 1) & ((c >> k) % 2 == 0)
                                  for k in range(1, LOGQ)], axis=1))
    put("identc", (r % QB) == j)
    put("level0", ((r % QB) // 2 == j // 2) & (j % 2 == 1) & (r % 2 == 0))
    put("diag", r // QB == c // QB)
    put("ones", 1.0)
    put("iota", np.arange(E)[None, :])
    put("headmask", r // XD == np.arange(XH)[None, :])
    return t


def need(eng, sem, count):
    if not isinstance(count, int) or count > 0:
        eng.wait_ge(sem, count)


def clear_semaphores(nc, sems):
    numbers = sorted(s.num for s in sems)
    runs, start = [], 0
    for i in range(1, len(numbers) + 1):
        if i == len(numbers) or numbers[i] != numbers[i - 1] + 1:
            runs.append(range(numbers[start], numbers[i - 1] + 1))
            start = i
    with nc.Block() as block:
        @block.sync
        def _(sp):
            for run in runs:
                sp.sem_clear(run)


class Room:

    def __init__(self, arena, start):
        self.arena, self.at = arena, start

    def take(self, *shape):
        n = 1
        for s in shape:
            n *= s
        v = self.arena[:, self.at:self.at + n]
        self.at += n
        assert self.at <= self.arena.shape[1], self.at
        if len(shape) == 2:
            v = v.rearrange("p (a b) -> p a b", b=shape[1])
        elif len(shape) == 3:
            v = v.rearrange("p (a b c) -> p a b c", b=shape[1], c=shape[2])
        elif len(shape) == 4:
            v = v.rearrange("p (a b c d) -> p a b c d", b=shape[1], c=shape[2], d=shape[3])
        return v


def halves(v):
    return v.rearrange("p b t -> p (b t)")


def build_prepare(nc, a, fixed, room, ps):
    x_sb = room.take(B, D)
    hn = room.take(B, D)
    wfa = room.take(KD, P)
    wga = room.take(KD, P)
    wfb = room.take(H)
    wb = room.take(KD, H)
    taps = room.take(3, P)
    ln1 = room.take(KD)
    alog = room.take(H)
    dtb = room.take(H)
    ea = room.take(H)
    lowf = room.take(TOK)
    stats = room.take(B, 6)
    mv = room.take(B, 2)
    sm = room.take(6, B)
    spt, sp1, spr = room.take(2, B, H), room.take(2, B, H), room.take(2, B, H)
    cexp = room.take(4)
    consts, x0, hT, lowg, heads = fixed["consts"], fixed["x0"], fixed["hT"], fixed["lowg"], fixed["heads"]

    def const(name):
        return consts[:, CONST[name][0]:CONST[name][1]]

    hps = ps[:, 0:2 * TOK].rearrange("p (k n) -> p k n", k=KD)
    tps = ps[:, 4 * HALF:4 * HALF + 3 * 64].rearrange("p (j r) -> p j r", j=3)
    fps = ps[:, 5 * HALF:7 * HALF]
    gps = ps[:, 0:TOK]
    zps = ps[:, 7 * HALF:7 * HALF + 2 * B * H].rearrange("p (s b h) -> p s b h", s=2, b=B)

    made = []
    with ExitStack() as ctx:
        def sem(name):
            made.append(ctx.enter_context(nc.semaphore(name)))
            return made[-1]

        x_in, w_in, c_in = sem("x_in"), sem("w_in"), sem("c_in")
        stat_made, rstd_made, h_made = sem("stat_made"), sem("rstd_made"), sem("h_made")
        hT_done, hT_made, taps_done = sem("hT_done"), sem("hT_made"), sem("taps_done")
        taps_made, lowf_done, lowf_made, small_done = sem("taps_made"), sem("lowf_done"), sem("lowf_made"), sem("small_done")
        lowg_done, decay_in, decay_sp, ea_made = sem("lowg_done"), sem("decay_in"), sem("decay_sp"), sem("ea_made")
        pool_step, vec_step, act_step = sem("pool_step"), sem("vec_step"), sem("act_step")
        block = ctx.enter_context(nc.Block())

        @block.sync
        def _(sp):
            sp.dma_start(x_sb, a["x"].rearrange("b t d -> t b d")).then_inc(x_in, 16)
            sp.dma_start(consts, a["consts"]).then_inc(c_in, 16)
            for dst, src in ((wfa, a["wfa"]), (wga, a["wga"]), (wb, a["wb"])):
                sp.dma_start(dst, src.rearrange("(k p) n -> p k n", p=P)).then_inc(w_in, 16)
            sp.dma_start(wfb, a["wfb"]).then_inc(w_in, 16)
            for j, name in enumerate(("conv_q", "conv_k", "conv_v")):
                sp.dma_start(taps[0:64, j, :], a[name].rearrange("i (h c) -> (i h) c", c=P)).then_inc(w_in, 16)
            sp.dma_start(alog, a["a_log"].partition_broadcast(P)).then_inc(w_in, 16)
            sp.dma_start(dtb, a["dt_bias"].partition_broadcast(P)).then_inc(w_in, 16)
            with nc.allow_non_contiguous_dma(reason="256 single weights, feature on partition"):
                for k in range(KD):
                    sp.dma_start(ln1[:, k:k + 1], a["ln1_w"].rearrange("(k p o) -> k p o", p=P, o=1)[k]).then_inc(w_in, 16)
            sp.dma_start(fixed["onw"], a["o_norm_w"].rearrange("(p o) -> p o", o=1)).then_inc(w_in, 16)
        W_ALL = 16 * 12

        @block.vector
        def _(dve):
            dve.wait_ge(x_in, 16)
            for b in range(B):
                nc.vector.bn_stats(stats[:, b, :], x_sb[:, b, :]).then_inc(vec_step, 1)
            for b in range(B):
                dve.wait_ge(vec_step, b + 1)
                nc.vector.bn_aggr(mv[:, b, :], stats[:, b, :]).then_inc(stat_made, 1)
            dve.wait_ge(rstd_made, 2)
            for b in range(B):
                nc.vector.tensor_scalar(x0[:, b, :], x_sb[:, b, :], mv[:, b, 0:1], sm[:, 0, b:b + 1],
                                        ALU.subtract, ALU.mult)
                nc.vector.tensor_scalar(hn[:, b, :], x_sb[:, b, :], mv[:, b, 0:1], sm[:, 4, b:b + 1],
                                        ALU.subtract, ALU.mult).then_inc(h_made, 1)
            dve.wait_ge(taps_done, 3)
            for j in range(3):
                nc.vector.tensor_copy(heads[:, :, 4 * j:4 * j + 4].rearrange("p h i -> p i h"),
                                      tps[:, j, :].rearrange("p (i h) -> p i h", i=4)).then_inc(taps_made, 1)
            dve.wait_ge(small_done, 1)
            nc.vector.tensor_tensor(spt[:, 0], zps[:, 0], dtb.unsqueeze(1).broadcast_to([P, B, H]), ALU.add).then_inc(decay_in, 1)
            nc.vector.tensor_scalar(spt[:, 1], zps[:, 1], -1.0, None, ALU.mult).then_inc(decay_in, 1)
            dve.wait_ge(decay_sp, 1)
            dve.wait_ge(act_step, 3)
            nc.vector.tensor_tensor(spt, sp1, spr, ALU.add).then_inc(vec_step, 1)
            dve.wait_ge(ea_made, 1)
            dve.wait_ge(vec_step, B + 1)
            nc.vector.scalar_tensor_tensor(heads[:, :, HT_G:HT_G + B].rearrange("p h b -> p b h"), spt[:, 0], -1.0,
                                           ea.unsqueeze(1).broadcast_to([P, B, H]), ALU.mult, ALU.mult)

        @block.gpsimd
        def _(pool):
            nc.gpsimd.memset(cexp[:, 0:1], -0.5).then_inc(pool_step, 1)
            nc.gpsimd.memset(fixed["mhalf"], -0.5).then_inc(pool_step, 1)
            pool.wait_ge(stat_made, B)
            pool.wait_ge(pool_step, 2)
            var = mv[:, :, 1]
            mh = cexp[:, 0:1].broadcast_to([P, B])
            nc.gpsimd.tensor_scalar(sm[:, 1, :], var, 1e-5, None, ALU.add).then_inc(pool_step, 1)
            pool.wait_ge(pool_step, 3)
            nc.gpsimd.tensor_tensor(sm[:, 0, :], sm[:, 1, :], mh, ALU.pow).then_inc(rstd_made, 1)
            pool.wait_ge(rstd_made, 1)
            nc.gpsimd.tensor_tensor(sm[:, 2, :], var, sm[:, 0, :], ALU.mult).then_inc(pool_step, 1)
            pool.wait_ge(pool_step, 4)
            nc.gpsimd.tensor_tensor(sm[:, 3, :], sm[:, 2, :], sm[:, 0, :], ALU.mult).then_inc(pool_step, 1)
            pool.wait_ge(pool_step, 5)
            nc.gpsimd.tensor_scalar(sm[:, 1, :], sm[:, 3, :], 1e-6, None, ALU.add).then_inc(pool_step, 1)
            pool.wait_ge(pool_step, 6)
            nc.gpsimd.tensor_tensor(sm[:, 5, :], sm[:, 1, :], mh, ALU.pow).then_inc(pool_step, 1)
            pool.wait_ge(pool_step, 7)
            nc.gpsimd.tensor_tensor(sm[:, 4, :], sm[:, 5, :], sm[:, 0, :], ALU.mult).then_inc(rstd_made, 1)

        @block.scalar
        def _(act):
            act.wait_ge(w_in, W_ALL)
            nc.scalar.activation(ea, alog, ACT.Exp).then_inc(ea_made, 1)
            act.wait_ge(hT_done, 1)
            for k in range(KD):
                nc.scalar.activation(hT[:, k, :], hps[:, k, :], ACT.Copy, scale=ln1[:, k:k + 1]).then_inc(hT_made, 1)
            act.wait_ge(lowf_done, 1)
            nc.scalar.activation(lowf, fps, ACT.Copy).then_inc(lowf_made, 1)
            act.wait_ge(lowg_done, 1)
            nc.scalar.activation(lowg, gps, ACT.Copy)
            act.wait_ge(decay_in, 2)
            nc.scalar.activation(sp1, spt, ACT.Abs).then_inc(act_step, 1)
            act.wait_ge(act_step, 1)
            nc.scalar.activation(sp1, sp1, ACT.Exp, scale=-1.0).then_inc(act_step, 1)
            nc.scalar.activation(spr, spt, ACT.Relu).then_inc(act_step, 1)
            act.wait_ge(act_step, 2)
            nc.scalar.activation(sp1, sp1, ACT.Ln, bias=1.0).then_inc(decay_sp, 1)
            act.wait_ge(vec_step, B + 1)
            nc.scalar.activation(heads[:, :, HT_SB:HT_SB + B].rearrange("p h b -> p b h"), spt[:, 1], ACT.Exp, scale=-0.5)

        @block.tensor
        def _(pe):
            pe.wait_ge(c_in, 16)
            pe.wait_ge(w_in, W_ALL)
            ident = const("ident")
            for j in range(3):
                nc.tensor.transpose(tps[:, j, :], taps[0:64, j, :], ident[0:64, 0:64]).then_inc(taps_done, 1)
            for b in range(B):
                pe.wait_ge(h_made, b + 1)
                for k in range(KD):
                    last = nc.tensor.transpose(hps[:, k, b * P:(b + 1) * P], hn[:, b, k * P:(k + 1) * P], ident)
            last.then_inc(hT_done, 1)
            pe.wait_ge(hT_made, KD)
            for w, dst, done in ((wfa, fps, lowf_done), (wga, gps, lowg_done)):
                for n in range(2):
                    for k in range(KD):
                        last = nc.tensor.matmul(dst[:, n * HALF:(n + 1) * HALF], w[:, k, :],
                                                hT[:, k, n * HALF:(n + 1) * HALF], start=(k == 0), stop=(k == KD - 1))
                last.then_inc(done, 1)
            pe.wait_ge(lowf_made, 1)
            for b in range(B):
                for k in range(KD):
                    nc.tensor.matmul(zps[:, 1, b, :], hT[:, k, b * P:(b + 1) * P], wb[:, k, :],
                                     start=(k == 0), stop=(k == KD - 1))
                last = nc.tensor.matmul(zps[:, 0, b, :], lowf[:, b * P:(b + 1) * P], wfb, start=True, stop=True)
            last.then_inc(small_done, 1)

    return made


def build_delta(nc, a, fixed, room, ps, wo, wo_in):
    consts, hT, lowg, heads, o_all = fixed["consts"], fixed["hT"], fixed["lowg"], fixed["heads"], fixed["o_all"]
    onw, mhalf = fixed["onw"], fixed["mhalf"]
    HB = B // 2
    SB = P // 2
    REFINE = 2

    def const(name):
        return consts[:, CONST[name][0]:CONST[name][1]]

    def half_words(*shape):
        n = 1
        for s in shape:
            n *= s
        v = room.take(n // 2).bitcast(F16)
        return v.rearrange("p (a b) -> p a b", b=shape[-1]) if len(shape) == 2 else v

    ident, incl, ones = const("ident"), const("incl"), const("ones")

    wqkv = room.take(3, KD, P)
    wg = room.take(P)
    small = room.take(HT)
    conv = [room.take(B, P) for _ in range(3)]
    gates = [room.take(B, P) for _ in range(2)]
    kp = room.take(B, P)
    dec = room.take(B, P)
    gm = room.take(B, P)
    rdiag = room.take(B, P)
    lt = [room.take(B, P) for _ in range(2)]
    pt = [room.take(B, P) for _ in range(2)]
    vp = [room.take(B, P) for _ in range(2)]
    at = room.take(B, P)
    rest = room.take(B, P)
    u = room.take(B, P)
    ot = room.take(B, P)
    sq = [room.take(B, P) for _ in range(3)]
    ksum, qsum, o_sum = room.take(B), room.take(B), room.take(B)
    rk = room.take(B)
    rq = [room.take(2, B) for _ in range(2)]
    ro = room.take(B)
    pw = room.take(7, B)

    l32 = half_words(B, P)
    yx = half_words(B, P)
    z7 = half_words(B, P)
    x6 = half_words(B, SB)
    y6 = half_words(B, SB)
    zc, xc = half_words(B, QB), half_words(B, QB)
    ltc = half_words(B, QB)
    c5 = half_words(B, QB)
    c6 = half_words(B, SB)
    y5 = half_words(B, QB)
    id16 = half_words(P)
    far16, after16 = half_words(P).bitcast(BF16), half_words(P).bitcast(BF16)
    v16 = half_words(B, P).bitcast(BF16)
    r16 = half_words(B, P).bitcast(BF16)

    pa, pb, pc, pd = [ps[:, 2 * HALF * i:2 * HALF * (i + 1)].rearrange("p (b t) -> p b t", b=B) for i in range(4)]
    yc = ps[:, 4 * HALF:4 * HALF + B * QB].rearrange("p (b j) -> p b j", b=B)
    dzc = ps[:, 5 * HALF:5 * HALF + B * QB].rearrange("p (b j) -> p b j", b=B)
    x6_ps = ps[:, 4 * HALF:5 * HALF].rearrange("p (b j) -> p b j", b=B)
    y6_ps = ps[:, 6 * HALF:7 * HALF].rearrange("p (b j) -> p b j", b=B)
    z6_ps = ps[:, 5 * HALF:6 * HALF].rearrange("p (b j) -> p b j", b=B)

    def blocks(v):
        return v.unsqueeze(2).broadcast_to([P, B, NQ, QB])

    def four(v):
        return v.rearrange("p b (q j) -> p b q j", q=NQ)

    def over_b(v, n):
        return v.unsqueeze(1).broadcast_to([P, B, n])

    def bank(v, n):
        return v[:, n * HB:(n + 1) * HB, :]

    made = []
    with ExitStack() as ctx:
        def sem(name):
            made.append(ctx.enter_context(nc.semaphore(name)))
            return made[-1]

        w_in = sem("head_w_in")
        small_made, fixed_made = sem("small_made"), sem("fixed_made")
        proj_done = [sem(f"{n}_proj_done") for n in ("q", "k", "v", "gate")]
        tap0_made = [sem(f"{n}_tap0_made") for n in "qkv"]
        conv_made = [sem(f"{n}_conv_made") for n in "qkv"]
        silu_made = [sem(f"{n}_silu_made") for n in ("q", "k", "v", "gate")]
        kt_done, ksum_made, qt_done, qsum_made = sem("kt_done"), sem("ksum_made"), sem("qt_done"), sem("qsum_made")
        rk_made, rq_made, rdiag_made, rkrep_done, kp_made = sem("rk_made"), sem("rq_made"), sem("rdiag_made"), sem("rkrep_done"), sem("kp_made")
        vt_done, vp_made, gm_made, diff_done = sem("vt_done"), sem("vp_made"), sem("gm_made"), sem("diff_done")
        exp_made, kk_done, qk_done = sem("exp_made"), sem("kk_done"), sem("qk_done")
        lt_made, pt_made, l32_made, ltc_made = sem("lt_made"), sem("pt_made"), sem("l32_made"), sem("ltc_made")
        at_made, c56_made, v16_made = sem("at_made"), sem("c56_made"), sem("v16_made")
        z_step = sem("z_step")
        x_made = sem("x_made")
        cx_done, yx_made, dz_done = sem("cx_done"), sem("yx_made"), sem("dz_done")
        zdiag_made, z5_made = sem("zdiag_made"), sem("z5_made")
        x6_done, x6_made, y6_done, y6_made = sem("x6_done"), sem("x6_made"), sem("y6_done"), sem("y6_made")
        z6_done, z6_made = sem("z6_done"), sem("z6_made")
        xr_done = sem("xr_done")
        u_made = sem("u_made")
        lu_done, rest_made, r_made = sem("lu_done"), sem("rest_made"), sem("r_made")
        o_done, osum_made, ro_made, ot_made = sem("o_done"), sem("osum_made"), sem("ro_made"), sem("ot_made")
        ott_done, head_made = sem("ott_done"), sem("head_made")
        pool_step, o_step = sem("norm_step"), sem("onorm_step")
        block = ctx.enter_context(nc.Block())
        XR = 2 + 2 * REFINE
        LU = 2 * REFINE

        def all_heads(eng, body):
            body(-1, 1, False, False, True)
            body(0, 0, False, True, True)
            body(1, 1, True, True, True)
            with eng.Fori(1, (H - 2) // 2) as i:
                body(i * 2, 0, True, True, True)
                body(i * 2 + 1, 1, True, True, True)
            body(H - 2, 0, True, True, True)
            body(H - 1, 1, True, True, False)
            body(H, 0, True, False, False)

        @block.sync
        def _(sp):
            def body(f):
                need(sp, proj_done[3], f)
                sp.nop(nofuse=True)
                for j, name in enumerate(("wq", "wk", "wv")):
                    sp.dma_start(wqkv[:, j], a[name].rearrange("(k p) (h c) -> h p k c", p=P, c=P)[f]).then_inc(w_in, 16)
                sp.dma_start(wg, a["wgb"].rearrange("p (h c) -> h p c", c=P)[f]).then_inc(w_in, 16)
            body(0)
            with sp.Fori(1, H) as f:
                body(f)
            split = wo[0].shape[1]
            w = a["wo"].rearrange("(h c) n -> c h n", c=P)
            sp.dma_start(wo[1], w[:, split:H, :]).then_inc(wo_in, 16)
            sp.wait_ge(proj_done[3], H)
            sp.dma_start(wo[0], w[:, 0:split, :]).then_inc(wo_in, 16)

        @block.tensor
        def _(pe):
            pe.wait_ge(fixed_made, 4)

            def project(j, f, n):
                dst = (pb, pa, pa)[j]
                for k in range(KD):
                    last = nc.tensor.matmul(halves(dst)[:, n * HALF:(n + 1) * HALF], wqkv[:, j, k, :],
                                            hT[:, k, n * HALF:(n + 1) * HALF], start=(k == 0), stop=(k == KD - 1))
                if n == 1:
                    last.then_inc(proj_done[j], 1)

            def each(dst, lhs, rhs, done, some=range(B)):
                for b in some:
                    last = nc.tensor.matmul(dst[:, b, :], lhs(b), rhs(b), start=True, stop=True)
                last.then_inc(done, 1)

            def transposed(dst, src, done):
                for b in range(B):
                    last = nc.tensor.transpose(dst[:, b, :], src[:, b, :], ident)
                last.then_inc(done, 1)

            def body(h, par, tail, back, front):
                f = h + 1

                def cx(k):
                    pe.wait_ge(x_made, 5 * h + k)
                    if k == 1:
                        pe.wait_ge(l32_made, h + 1)
                    each(yc, lambda b: l32[:, b, :], lambda b: xc[:, b, :], cx_done)

                def dz(k):
                    pe.wait_ge(yx_made, 5 * h + k)
                    each(dzc, lambda b: yx[:, b, :], lambda b: zc[:, b, :], dz_done)

                def pairs(dst, dq, lhs, rhs, lq, done):
                    for b in range(B):
                        for q in (0, 2):
                            i, o = slice((lq + q) * QB, (lq + q + 1) * QB), slice((dq + q) * QB, (dq + q + 1) * QB)
                            last = nc.tensor.matmul(dst[o, b, :], lhs[i, b, :], rhs[i, b, :], start=True, stop=True,
                                                    tile_position=((lq + q) * QB, (dq + q) * QB))
                    last.then_inc(done, 1)

                def gates_proj():
                    pe.wait_ge(conv_made[0], 3 * f + 3)
                    for n in range(2):
                        last = nc.tensor.matmul(halves(pb)[:, n * HALF:(n + 1) * HALF], wg,
                                                lowg[:, n * HALF:(n + 1) * HALF], start=True, stop=True)
                    last.then_inc(proj_done[3], 1)

                def lu(step):
                    if step == 0:
                        pe.wait_ge(at_made, h + 1)
                    for n in range(2):
                        pe.wait_ge(u_made, XR * h + 2 * step + n + 1)
                        each(pd, lambda b: at[:, b, :], lambda b: u[:, b, :], lu_done, range(n * HB, (n + 1) * HB))

                def correct(step):
                    for n in range(2):
                        pe.wait_ge(r_made, LU * h + 2 * step + n + 1)
                        each(pc, lambda b: z7[:, b, :], lambda b: r16[:, b, :], xr_done, range(n * HB, (n + 1) * HB))

                if back:
                    cx(1)
                if front:
                    pe.wait_ge(w_in, 64 * f + 64)
                    need(pe, lt_made, f)
                    project(1, f, 0)
                if back:
                    dz(1)
                if front:
                    project(1, f, 1)
                if back:
                    cx(2)
                if front:
                    need(pe, pt_made, f)
                    project(0, f, 0)
                if back:
                    dz(2)
                if front:
                    project(0, f, 1)
                if back:
                    cx(3)
                if tail:
                    pe.wait_ge(ot_made, h)
                    transposed(pd, ot, ott_done)
                if back:
                    dz(3)
                if front:
                    pe.wait_ge(conv_made[1], 3 * f + 3)
                    project(2, f, 0)
                if back:
                    cx(4)
                if front:
                    project(2, f, 1)
                if back:
                    dz(4)
                    pe.wait_ge(x_made, 5 * h + 5)
                    pe.wait_ge(c56_made, h + 1)
                    pe.nop(nofuse=True)
                    pairs(yc, 1, c5, xc, 0, cx_done)
                if front:
                    gates_proj()
                if back:
                    pe.wait_ge(yx_made, 5 * h + 5)
                    pe.nop(nofuse=True)
                    pairs(dzc, 0, y5, zc, 1, dz_done)
                    pe.wait_ge(zdiag_made, h + 1)
                    pe.wait_ge(z5_made, h + 1)
                    pe.nop(nofuse=True)
                    each(x6_ps[0:SB], lambda b: z7[0:SB, b, 0:SB], lambda b: id16[0:SB, 0:SB], x6_done)
                    pe.wait_ge(x6_made, h + 1)
                    need(pe, head_made, h)
                    pe.nop(nofuse=True)
                    each(y6_ps[SB:P], lambda b: c6[0:SB, b, :], lambda b: x6[0:SB, b, :], y6_done)
                if front:
                    pe.wait_ge(silu_made[1], f + 1)
                    pe.wait_ge(silu_made[3], f + 1)
                    transposed(pb, conv[1], kt_done)
                if back:
                    pe.wait_ge(y6_made, h + 1)
                    pe.nop(nofuse=True)
                    each(z6_ps[0:SB], lambda b: y6[SB:P, b, :], lambda b: z7[SB:P, b, SB:P], z6_done)
                    pe.wait_ge(z6_made, h + 1)
                    pe.wait_ge(v16_made, h + 1)
                    for n in range(2):
                        each(pc, lambda b: z7[:, b, :], lambda b: v16[:, b, :], xr_done, range(n * HB, (n + 1) * HB))
                if front:
                    pe.wait_ge(silu_made[2], f + 1)
                    transposed(pa, conv[2], vt_done)
                    pe.wait_ge(ksum_made, f + 1)
                    pe.wait_ge(silu_made[0], f + 1)
                    transposed(pb, conv[0], qt_done)
                if back:
                    lu(0)
                if front:
                    pe.wait_ge(vp_made, f + 1)
                    pe.wait_ge(gm_made, f + 1)
                    for n in range(2):
                        nc.tensor.matmul(halves(pa)[:, n * HALF:(n + 1) * HALF], far16,
                                         after16.unsqueeze(1).broadcast_to([P, HB, P]), start=True, stop=False)
                        last = nc.tensor.matmul(halves(pa)[:, n * HALF:(n + 1) * HALF], const("strict"),
                                                halves(gm)[:, n * HALF:(n + 1) * HALF], start=False, stop=True)
                    last.then_inc(diff_done, 1)
                if back:
                    correct(0)
                if front:
                    pe.wait_ge(rdiag_made, f + 1)
                    pe.wait_ge(qsum_made, f + 1)
                    for n in range(2):
                        last = nc.tensor.matmul(halves(pb)[:, n * HALF:(n + 1) * HALF], ones,
                                                halves(rdiag)[:, n * HALF:(n + 1) * HALF], start=True, stop=True)
                    last.then_inc(rkrep_done, 1)
                if back:
                    lu(1)
                if front:
                    pe.wait_ge(kp_made, f + 1)
                    pe.wait_ge(exp_made, f + 1)
                    each(pa, lambda b: kp[:, b, :], lambda b: kp[:, b, :], kk_done)
                if back:
                    correct(1)
                if front:
                    each(pb, lambda b: kp[:, b, :], lambda b: conv[0][:, b, :], qk_done)
                if back:
                    for b in range(B):
                        if b % HB == 0:
                            pe.wait_ge(u_made, XR * h + XR - 1 + b // HB)
                        last = nc.tensor.matmul(pd[:, b, :], pt[par][:, b, :], u[:, b, :], start=True, stop=True)
                    last.then_inc(o_done, 1)

            all_heads(pe, body)

        @block.scalar
        def _(act):
            def tap0(j, f):
                act.wait_ge(proj_done[j], f + 1)
                act.wait_ge(small_made, f + 1)
                need(act, (qk_done, kp_made, vt_done)[j], f)
                nc.scalar.activation(halves(conv[j]), halves((pb, pa, pa)[j]), ACT.Copy,
                                     scale=small[:, 4 * j + 3:4 * j + 4]).then_inc(tap0_made[j], 1)

            def silu(j, f):
                act.wait_ge(conv_made[j], 3 * f + 3)
                nc.scalar.activation(halves(conv[j]), halves(conv[j]), ACT.Silu).then_inc(silu_made[j], 1)

            def squares(src, scrap, total, summed):
                for b in range(B):
                    last = nc.scalar.activation(scrap[:, b, :], src[:, b, :], ACT.Square, accum_out=total[:, b:b + 1])
                last.then_inc(summed, 1)

            def body(h, par, tail, back, front):
                f = h + 1
                fpar = 1 - par
                if back:
                    act.wait_ge(lt_made, h + 1)
                    need(act, x_made, 5 * h)
                    for q in range(NQ):
                        s = slice(q * QB, (q + 1) * QB)
                        last = nc.scalar.activation(ltc[s], lt[par][s, :, s], ACT.Copy)
                    last.then_inc(ltc_made, 1)
                if tail:
                    act.wait_ge(o_done, h)
                    need(act, ro_made, h - 1)
                    squares(pd, sq[2], o_sum, osum_made)
                if front:
                    tap0(1, f)
                    tap0(0, f)
                if back:
                    need(act, y6_done, h)
                    for q in (0, 2):
                        s, t = slice(q * QB, (q + 1) * QB), slice((q + 1) * QB, (q + 2) * QB)
                        nc.scalar.activation(c5[s], lt[par][s, :, t], ACT.Copy)
                    nc.scalar.activation(c6[0:SB], lt[par][0:SB, :, SB:P], ACT.Copy).then_inc(c56_made, 1)
                if front:
                    silu(1, f)
                    tap0(2, f)
                if back:
                    need(act, xr_done, XR * h)
                    act.wait_ge(vp_made, h + 1)
                    nc.scalar.activation(halves(v16), halves(vp[par]), ACT.Copy).then_inc(v16_made, 1)
                if front:
                    silu(0, f)
                    act.wait_ge(proj_done[3], f + 1)
                    need(act, head_made, h)
                    nc.scalar.activation(halves(gates[fpar]), halves(pb), ACT.Silu).then_inc(silu_made[3], 1)
                if back:
                    act.wait_ge(x_made, 5 * h + 5)
                    for q in range(NQ):
                        s = slice(q * QB, (q + 1) * QB)
                        last = nc.scalar.activation(z7[s, :, s], zc[s], ACT.Copy)
                    last.then_inc(zdiag_made, 1)
                    act.wait_ge(x6_done, h + 1)
                    nc.scalar.activation(halves(x6)[0:SB], halves(x6_ps)[0:SB], ACT.Copy).then_inc(x6_made, 1)
                    act.wait_ge(y6_done, h + 1)
                    nc.scalar.activation(halves(y6)[SB:P], halves(y6_ps)[SB:P], ACT.Copy).then_inc(y6_made, 1)
                if front:
                    silu(2, f)
                    act.wait_ge(kt_done, f + 1)
                    need(act, rk_made, f)
                    squares(pb, sq[0], ksum, ksum_made)
                if back:
                    for n in range(2):
                        act.wait_ge(xr_done, XR * h + n + 1)
                        nc.scalar.activation(bank(u, n), bank(pc, n), ACT.Copy).then_inc(u_made, 1)
                if front:
                    act.wait_ge(qt_done, f + 1)
                    need(act, rq_made, f)
                    squares(pb, sq[1], qsum, qsum_made)
                    act.wait_ge(diff_done, f + 1)
                    need(act, pt_made, f)
                    nc.scalar.activation(halves(dec), halves(pa), ACT.Exp).then_inc(exp_made, 1)

            all_heads(act, body)

        @block.vector
        def _(dve):
            def tap(j, f, shift):
                if shift == 1:
                    dve.wait_ge(tap0_made[j], f + 1)
                else:
                    dve.wait_ge(conv_made[j], 3 * f + shift - 1)
                nc.vector.scalar_tensor_tensor(conv[j][:, :, shift:], (pb, pa, pa)[j][:, :, :P - shift],
                                               small[:, 4 * j + 3 - shift:4 * j + 4 - shift], conv[j][:, :, shift:],
                                               ALU.mult, ALU.add).then_inc(conv_made[j], 1)

            def body(h, par, tail, back, front):
                f = h + 1
                fpar = 1 - par

                def to_x(k):
                    dve.wait_ge(z_step, 6 * h + k + 1)
                    nc.vector.transpose(xc.rearrange("p b j -> p (b j)"), zc.rearrange("p b j -> p (b j)")).then_inc(x_made, 1)

                def expand(k):
                    dve.wait_ge(cx_done, 5 * h + k)
                    nc.vector.tensor_tensor(four(yx), blocks(yc),
                                            const("ylevel").rearrange("p (k q j) -> p k q j", q=NQ, j=QB)[:, k - 1]
                                            .unsqueeze(1).broadcast_to([P, B, NQ, QB]), ALU.mult).then_inc(yx_made, 1)

                def update(k):
                    dve.wait_ge(dz_done, 5 * h + k)
                    nc.vector.tensor_tensor(zc, zc, dzc, ALU.subtract).then_inc(z_step, 1)
                    to_x(k + 1)

                def residual(step):
                    for n in range(2):
                        dve.wait_ge(lu_done, LU * h + 2 * step + n + 1)
                        dve.wait_ge(rest_made, LU * h + 2 * step + n + 1)
                        nc.vector.tensor_tensor(bank(r16, n), bank(rest, n), bank(pd, n), ALU.subtract).then_inc(r_made, 1)

                def corrected(step):
                    for n in range(2):
                        dve.wait_ge(xr_done, XR * h + 2 * step + n + 3)
                        nc.vector.tensor_tensor(bank(u, n), bank(u, n), bank(pc, n), ALU.add).then_inc(u_made, 1)

                if back:
                    dve.wait_ge(ltc_made, h + 1)
                    need(dve, zdiag_made, h)
                    nc.vector.tensor_tensor(zc, ltc, over_b(const("level0"), QB), ALU.mult).then_inc(z_step, 1)
                    dve.wait_ge(z_step, 6 * h + 1)
                    nc.vector.tensor_tensor(zc, over_b(const("identc"), QB), zc, ALU.subtract).then_inc(z_step, 1)
                    to_x(1)
                    expand(1)
                    update(1)
                    expand(2)
                if front:
                    tap(1, f, 1)
                if back:
                    update(2)
                if tail:
                    dve.wait_ge(ro_made, h)
                    nc.vector.tensor_tensor(ot, pd, ro.unsqueeze(2).broadcast_to([P, B, P]), ALU.mult).then_inc(ot_made, 1)
                if front:
                    tap(1, f, 2)
                if back:
                    expand(3)
                if front:
                    tap(1, f, 3)
                if back:
                    update(3)
                if front:
                    tap(0, f, 1)
                if back:
                    expand(4)
                if front:
                    tap(0, f, 2)
                if back:
                    update(4)
                if tail:
                    dve.wait_ge(ott_done, h)
                    dve.wait_ge(silu_made[3], h)
                    nc.vector.scalar_tensor_tensor(o_all[:, h - 1, :], halves(pd), onw, halves(gates[fpar]),
                                                   ALU.mult, ALU.mult).then_inc(head_made, 1)
                if front:
                    tap(0, f, 3)
                if back:
                    dve.wait_ge(cx_done, 5 * h + 5)
                    nc.vector.tensor_copy(y5, yc).then_inc(yx_made, 1)
                if front:
                    tap(2, f, 1)
                if back:
                    dve.wait_ge(dz_done, 5 * h + 5)
                    for q in (0, 2):
                        s, t = slice(q * QB, (q + 1) * QB), slice((q + 1) * QB, (q + 2) * QB)
                        last = nc.vector.tensor_scalar(z7[s, :, t], dzc[s], -1.0, None, ALU.mult)
                    last.then_inc(z5_made, 1)
                if front:
                    tap(2, f, 2)
                    tap(2, f, 3)
                if back:
                    dve.wait_ge(z6_done, h + 1)
                    nc.vector.tensor_scalar(z7[0:SB, :, SB:P], z6_ps[0:SB], -1.0, None, ALU.mult).then_inc(z6_made, 1)
                if front:
                    dve.wait_ge(vt_done, f + 1)
                    nc.vector.tensor_tensor(vp[fpar], pa, small[:, HT_SB:HT_SB + B].unsqueeze(2).broadcast_to([P, B, P]),
                                            ALU.mult).then_inc(vp_made, 1)
                if back:
                    residual(0)
                    corrected(0)
                if front:
                    dve.wait_ge(rkrep_done, f + 1)
                    nc.vector.tensor_tensor(halves(kp), halves(conv[1]), halves(pb), ALU.mult).then_inc(kp_made, 1)
                if back:
                    residual(1)
                if front:
                    dve.wait_ge(kk_done, f + 1)
                    dve.wait_ge(exp_made, f + 1)
                    if not (isinstance(f, int) and f < 2):
                        dve.wait_ge(at_made, f - 1)
                        dve.wait_ge(c56_made, f - 1)
                    nc.vector.tensor_tensor(halves(lt[fpar]), halves(pa), halves(dec), ALU.mult).then_inc(lt_made, 1)
                if back:
                    corrected(1)
                if front:
                    dve.wait_ge(qk_done, f + 1)
                    nc.vector.tensor_tensor(halves(pt[fpar]), halves(pb), halves(dec), ALU.mult).then_inc(pt_made, 1)

            all_heads(dve, body)

        @block.gpsimd
        def _(pool):
            mh = mhalf.broadcast_to([P, B])
            nc.gpsimd.memset(halves(z7), 0.0).then_inc(fixed_made, 1)
            nc.gpsimd.tensor_copy(id16, ident).then_inc(fixed_made, 1)
            nc.gpsimd.tensor_scalar(far16, ident, -30000.0, None, ALU.mult).then_inc(fixed_made, 1)
            nc.gpsimd.tensor_copy(after16, const("strict")).then_inc(fixed_made, 1)

            def body(h, par, tail, back, front):
                f = h + 1
                fpar = 1 - par

                def leave(step):
                    for n in range(2):
                        pool.wait_ge(u_made, XR * h + 2 * step + n + 1)
                        nc.gpsimd.tensor_tensor(bank(rest, n), bank(vp[par], n), bank(u, n), ALU.subtract).then_inc(rest_made, 1)

                if front:
                    need(pool, conv_made[2], 3 * f)
                    need(pool, vp_made, f)
                    pool.nop(nofuse=True)
                    nc.gpsimd.tensor_copy(small, heads[:, f, :]).then_inc(small_made, 1)
                if back:
                    pool.wait_ge(lt_made, h + 1)
                    need(pool, cx_done, 5 * h)
                    nc.gpsimd.tensor_tensor(l32, lt[par], over_b(const("diag"), P), ALU.mult).then_inc(l32_made, 1)
                if tail:
                    pool.wait_ge(osum_made, h)
                    pool.wait_ge(rq_made, h)
                    need(pool, ot_made, h - 1)
                    nc.gpsimd.tensor_tensor(pw[:, 4, :], o_sum, rq[fpar][:, 1, :], ALU.mult).then_inc(o_step, 1)
                    pool.wait_ge(o_step, 3 * h - 2)
                    pool.nop(nofuse=True)
                    nc.gpsimd.tensor_scalar(pw[:, 5, :], pw[:, 4, :], 1.0 / P, 1e-6, ALU.mult, ALU.add).then_inc(o_step, 1)
                    pool.wait_ge(o_step, 3 * h - 1)
                    nc.gpsimd.tensor_tensor(pw[:, 6, :], pw[:, 5, :], mh, ALU.pow).then_inc(o_step, 1)
                    pool.wait_ge(o_step, 3 * h)
                    nc.gpsimd.tensor_tensor(ro, pw[:, 6, :], rq[fpar][:, 0, :], ALU.mult).then_inc(ro_made, 1)
                if back:
                    need(pool, lu_done, LU * h)
                    nc.gpsimd.tensor_tensor(at, lt[par], over_b(const("before"), P), ALU.mult).then_inc(at_made, 1)
                if front:
                    pool.wait_ge(small_made, f + 1)
                    need(pool, diff_done, f)
                    nc.gpsimd.tensor_tensor(gm, over_b(incl, P), small[:, HT_G:HT_G + B].unsqueeze(2).broadcast_to([P, B, P]),
                                            ALU.mult).then_inc(gm_made, 1)
                    pool.wait_ge(ksum_made, f + 1)
                    n0 = 5 * f
                    pool.nop(nofuse=True)
                    nc.gpsimd.tensor_scalar(pw[:, 0, :], ksum, 1e-6, None, ALU.add).then_inc(pool_step, 1)
                    pool.wait_ge(pool_step, n0 + 1)
                    nc.gpsimd.tensor_tensor(pw[:, 1, :], pw[:, 0, :], mh, ALU.pow).then_inc(pool_step, 1)
                    pool.wait_ge(pool_step, n0 + 2)
                    nc.gpsimd.tensor_tensor(rk, pw[:, 1, :], small[:, HT_SB:HT_SB + B], ALU.mult).then_inc(rk_made, 1)
                if back:
                    leave(0)
                if front:
                    pool.wait_ge(rk_made, f + 1)
                    need(pool, rkrep_done, f)
                    nc.gpsimd.tensor_tensor(rdiag, over_b(ident, P), rk.unsqueeze(2).broadcast_to([P, B, P]),
                                            ALU.mult).then_inc(rdiag_made, 1)
                if back:
                    leave(1)
                if front:
                    pool.wait_ge(qsum_made, f + 1)
                    pool.nop(nofuse=True)
                    nc.gpsimd.tensor_scalar(pw[:, 2, :], qsum, 1e-6, None, ALU.add).then_inc(pool_step, 1)
                    pool.wait_ge(pool_step, n0 + 3)
                    nc.gpsimd.tensor_tensor(pw[:, 3, :], pw[:, 2, :], mh, ALU.pow).then_inc(pool_step, 1)
                    pool.wait_ge(pool_step, n0 + 4)
                    pool.nop(nofuse=True)
                    nc.gpsimd.tensor_scalar(rq[fpar][:, 0, :], pw[:, 3, :], float(P) ** -0.5, None, ALU.mult).then_inc(pool_step, 1)
                    pool.wait_ge(pool_step, n0 + 5)
                    nc.gpsimd.tensor_tensor(rq[fpar][:, 1, :], rq[fpar][:, 0, :], rq[fpar][:, 0, :], ALU.mult).then_inc(rq_made, 1)

            all_heads(pool, body)

    return made


def build_mlp(nc, a, fixed, room, ps, wo, wo_in):
    consts, x0, o_all, x1 = fixed["consts"], fixed["x0"], fixed["o_all"], fixed["x1"]
    ident = consts[:, CONST["ident"][0]:CONST["ident"][1]]
    w_gate = room.take(KD, I1)
    w_up = room.take(KD, I1)
    w_down = room.take(NI, D)
    xr = room.take(B, D)
    xa = room.take(B, D)
    h2 = room.take(B, D)
    sqr = room.take(D)
    h2T = room.take(KD, TOK)
    mT = room.take(NI, TOK)
    sg = [room.take(TOK) for _ in range(2)]
    ln2 = room.take(KD)
    ms, rms = room.take(B), room.take(B)
    tmp = room.take(B)

    with ExitStack() as ctx:
        def sem(name):
            return ctx.enter_context(nc.semaphore(name))

        w_in, x_in = sem("mlp_w_in"), sem("x_again_in")
        oproj_done, xa_made, xr_made, ms_made, rms_made = sem("oproj_done"), sem("xa_made"), sem("xr_made"), sem("ms_made"), sem("rms_made")
        h2_made, h2T_done, h2T_made = sem("h2_made"), sem("h2T_done"), sem("h2T_made")
        gate_done, up_done, sg_made, m_made = sem("gate_done"), sem("up_done"), sem("sg_made"), sem("m_made")
        down_done, pool_step = sem("down_done"), sem("rms_step")
        block = ctx.enter_context(nc.Block())

        @block.sync
        def _(sp):
            sp.dma_start(w_gate, a["w_gate"].rearrange("(k p) n -> p k n", p=P)).then_inc(w_in, 16)
            sp.dma_start(w_up, a["w_up"].rearrange("(k p) n -> p k n", p=P)).then_inc(w_in, 16)
            sp.dma_start(w_down, a["w_down"].rearrange("(c p) n -> p c n", p=P)).then_inc(w_in, 16)
            sp.dma_start(xr, a["x"].rearrange("b t d -> t b d")).then_inc(x_in, 16)
            with nc.allow_non_contiguous_dma(reason="256 single weights, feature on partition"):
                for k in range(KD):
                    sp.dma_start(ln2[:, k:k + 1], a["ln2_w"].rearrange("(k p o) -> k p o", p=P, o=1)[k]).then_inc(x_in, 16)

        def tok_cols(b):
            return ps[:, b * D:(b + 1) * D]

        def gate_ps(c):
            return ps[:, (c % 2) * 2 * TOK:(c % 2) * 2 * TOK + TOK]

        def up_ps(c):
            return ps[:, (c % 2) * 2 * TOK + TOK:(c % 2) * 2 * TOK + 2 * TOK]

        hps = ps[:, 2 * TOK:4 * TOK].rearrange("p (k n) -> p k n", k=KD)

        @block.tensor
        def _(pe):
            pe.wait_ge(wo_in, 32)
            split = wo[0].shape[1]
            for b in range(B):
                for h in range(H):
                    last = nc.tensor.matmul(tok_cols(b), o_all[:, h, b * P:(b + 1) * P],
                                            wo[0][:, h, :] if h < split else wo[1][:, h - split, :],
                                            start=(h == 0), stop=(h == H - 1))
                if b % 2:
                    last.then_inc(oproj_done, 1)
            for b in range(B):
                pe.wait_ge(h2_made, b + 1)
                for k in range(KD):
                    last = nc.tensor.transpose(hps[:, k, b * P:(b + 1) * P], h2[:, b, k * P:(k + 1) * P], ident)
            last.then_inc(h2T_done, 1)
            pe.wait_ge(h2T_made, KD)
            pe.wait_ge(w_in, 48)
            for c in range(NI):
                if c >= 2:
                    pe.wait_ge(m_made, c - 1)
                for w, dst, done in ((w_gate, gate_ps(c), gate_done), (w_up, up_ps(c), up_done)):
                    for n in range(2):
                        for k in range(KD):
                            last = nc.tensor.matmul(dst[:, n * HALF:(n + 1) * HALF], w[:, k, c * P:(c + 1) * P],
                                                    h2T[:, k, n * HALF:(n + 1) * HALF], start=(k == 0), stop=(k == KD - 1))
                    last.then_inc(done, 1)
            pe.wait_ge(m_made, NI)
            for b in range(B):
                for c in range(NI):
                    last = nc.tensor.matmul(tok_cols(b), mT[:, c, b * P:(b + 1) * P], w_down[:, c, :],
                                            start=(c == 0), stop=(c == NI - 1))
                if b % 2:
                    last.then_inc(down_done, 1)

        @block.vector
        def _(dve):
            for b in range(B):
                if b % 2 == 0:
                    dve.wait_ge(oproj_done, b // 2 + 1)
                nc.vector.tensor_tensor(xa[:, b, :], x0[:, b, :], tok_cols(b), ALU.add).then_inc(xa_made, 1)
            dve.wait_ge(rms_made, 1)
            for b in range(B):
                nc.vector.tensor_scalar(h2[:, b, :], xa[:, b, :], rms[:, b:b + 1], None, ALU.mult).then_inc(h2_made, 1)
            for c in range(NI):
                dve.wait_ge(sg_made, c + 1)
                dve.wait_ge(up_done, c + 1)
                nc.vector.tensor_tensor(mT[:, c, :], sg[c % 2], up_ps(c), ALU.mult).then_inc(m_made, 1)
            dve.wait_ge(xr_made, 1)
            for b in range(0, B, 2):
                dve.wait_ge(down_done, b // 2 + 1)
                nc.vector.tensor_tensor(x1[:, b:b + 2, :].rearrange("p b d -> p (b d)"),
                                        xr[:, b:b + 2, :].rearrange("p b d -> p (b d)"), ps[:, b * D:(b + 2) * D], ALU.add)

        @block.scalar
        def _(act):
            for b in range(B):
                act.wait_ge(xa_made, b + 1)
                if b:
                    act.wait_ge(ms_made, b)
                nc.scalar.activation(sqr, xa[:, b, :], ACT.Square, accum_out=ms[:, b:b + 1]).then_inc(ms_made, 1)
            act.wait_ge(x_in, 48)
            act.wait_ge(h2T_done, 1)
            for k in range(KD):
                nc.scalar.activation(h2T[:, k, :], hps[:, k, :], ACT.Copy, scale=ln2[:, k:k + 1]).then_inc(h2T_made, 1)
            for c in range(NI):
                act.wait_ge(gate_done, c + 1)
                if c >= 2:
                    act.wait_ge(m_made, c - 1)
                nc.scalar.activation(sg[c % 2], gate_ps(c), ACT.Silu).then_inc(sg_made, 1)

        @block.gpsimd
        def _(pool):
            pool.wait_ge(ms_made, B)
            nc.gpsimd.tensor_scalar(tmp, ms, 1.0 / D, 1e-6, ALU.mult, ALU.add).then_inc(pool_step, 1)
            pool.wait_ge(pool_step, 1)
            nc.gpsimd.tensor_tensor(rms, tmp, fixed["mhalf"].broadcast_to([P, B]), ALU.pow).then_inc(rms_made, 1)
            pool.wait_ge(x_in, 48)
            nc.gpsimd.tensor_tensor(xr, xr, xa, ALU.add).then_inc(xr_made, 1)


def layernorm_stats(nc, dve, pool_like, x, stats, mv, done, step):
    for b in range(B):
        nc.vector.bn_stats(stats[:, b, :], x[:, b, :]).then_inc(step, 1)
    for b in range(B):
        dve.wait_ge(step, b + 1)
        nc.vector.bn_aggr(mv[:, b, :], stats[:, b, :]).then_inc(done, 1)


def gate_up_loads(sp, a, ring, g, slot, arrived):
    wgu = ring["wgu"][slot]
    for j, name in enumerate(("e_gate", "e_up")):
        for k in range(KD):
            sp.dma_start(wgu[:, :, k, j * I2:(j + 1) * I2],
                         a[name].rearrange("(g e) (p k) n -> g k p e n", e=GRP, k=KD)[g, k]).then_inc(arrived, 16)


def down_load(sp, a, ring, g, slot, arrived):
    wd = ring["wd"][slot]
    sp.dma_start(wd[0:IH], a["e_down"].rearrange("(g e) (p c) n -> g p e (c n)", e=GRP, c=2)[g]
                 .rearrange("p e (c n) -> p e c n", c=2)).then_inc(arrived, 16)


LOADS = 5 * 16


def build_cross(nc, a, fixed, room, ps, ring, ring_in, scratch):
    consts, x1, mhalf = fixed["consts"], fixed["x1"], fixed["mhalf"]
    ident = consts[:, CONST["ident"][0]:CONST["ident"][1]]
    headmask = consts[:, CONST["headmask"][0]:CONST["headmask"][1]]
    NJ = XH // 2
    yq = room.take(B, D)
    stats, mv = room.take(B, 6), room.take(B, 2)
    r1, r2, r3 = room.take(B), room.take(B), room.take(B)
    gam = room.take(1)
    yb = [room.take(D) for _ in range(2)]
    cb = [room.take(D) for _ in range(2)]
    cm = [room.take(XH, D) for _ in range(2)]
    cT = [room.take(2, XH, XD + 1) for _ in range(2)]
    pr = [room.take(2, D) for _ in range(2)]
    prT = [room.take(2, 2, P) for _ in range(2)]
    nmax = room.take(2, 2)
    zeros = room.take(D)
    ret = room.take(2, XH, XD)
    rec = room.take(2, XH, 1)

    def bank(i):
        return ps[:, i * HALF:(i + 1) * HALF]

    res_ps = bank(4)[:, 0:2 * XH * (XD + 1)].rearrange("p (q h c) -> p q h c", q=2, h=XH)
    cT_ps = bank(5)[:, 0:2 * P].rearrange("p (l h c) -> p l h c", l=2, h=XH)
    rT_ps = bank(6)[:, 0:D]
    NU = NJ * 2

    with ExitStack() as ctx:
        def sem(name):
            return ctx.enter_context(nc.semaphore(name))

        stat_step, stat_made, r_step, r_made, yq_made = sem("xstat_step"), sem("xstat_made"), sem("xr_step"), sem("xr_made"), sem("yq_made")
        gam_in, cb_in, yb_made, cm_made = sem("gam_in"), [sem(f"ctx_in{i}") for i in range(2)], sem("yb_made"), sem("cm_made")
        cT_done, cT_made, ones_made = sem("cT_done"), sem("cT_made"), sem("cT_ones_made")
        s_done, max_made, exp_made, pT_done, pT_made, res_done = sem("score_done"), sem("max_made"), sem("xexp_made"), sem("pT_done"), sem("pT_made"), sem("res_done")
        rec_made, ret_made, rT_done, x2_made = sem("rec_made"), sem("ret_made"), sem("rT_done"), sem("x2_made")
        zeros_made, zeros_out = sem("zeros_made"), sem("zeros_out")
        block = ctx.enter_context(nc.Block())

        def sequences(eng, body):
            body(0, 0, False)
            body(1, 1, False)
            with eng.Fori(1, B // 2 - 1) as i:
                body(i * 2, 0, False)
                body(i * 2 + 1, 1, False)
            body(B - 2, 0, False)
            body(B - 1, 1, True)

        @block.sync
        def _(sp):
            sp.dma_start(gam, a["gamma"].partition_broadcast(P)).then_inc(gam_in, 16)

            def load(b, par):
                if not (isinstance(b, int) and b < 2):
                    sp.wait_ge(cm_made, 2 * b - 2)
                    sp.nop(nofuse=True)
                    sp.wait_ge(cT_done, b - 1)
                    sp.nop(nofuse=True)
                sp.dma_start(cb[par], a["ctx"][b]).then_inc(cb_in[par], 16)
            load(0, 0)
            load(1, 1)
            for g in range(RING):
                gate_up_loads(sp, a, ring, g, g, ring_in[g])
                down_load(sp, a, ring, g, g, ring_in[g])
            with sp.Fori(1, B // 2) as i:
                load(i * 2, 0)
                load(i * 2 + 1, 1)
            sp.wait_ge(zeros_made, 1)
            sp.dma_start(scratch["rows"].rearrange("(g p) d -> p g d", p=P),
                         zeros.unsqueeze(1).broadcast_to([P, SLOTS // P, D])).then_inc(zeros_out, 16)
            sp.dma_start(scratch["results"][SLOTS:SLOTS + 1], zeros[0:1]).then_inc(zeros_out, 16)
            sp.wait_ge(zeros_out, 32)

        @block.gpsimd
        def _(pool):
            nc.gpsimd.memset(zeros, 0.0).then_inc(zeros_made, 1)
            for par in range(2):
                nc.gpsimd.memset(cT[par][:, :, :, XD:XD + 1], 1.0).then_inc(ones_made, 1)
            pool.wait_ge(stat_made, B)
            nc.gpsimd.tensor_scalar(r1, mv[:, :, 1], 1e-5, None, ALU.add).then_inc(r_step, 1)
            pool.wait_ge(r_step, 1)
            nc.gpsimd.tensor_tensor(r2, r1, mhalf.broadcast_to([P, B]), ALU.pow).then_inc(r_step, 1)
            pool.wait_ge(r_step, 2)
            nc.gpsimd.tensor_scalar(r3, r2, XD ** -0.5, None, ALU.mult).then_inc(r_made, 1)

            def body(b, par):
                if not (isinstance(b, int) and b < 2):
                    pool.wait_ge(s_done, NU * b - NU)
                pool.wait_ge(yq_made, B)
                pool.nop(nofuse=True)
                nc.gpsimd.tensor_copy(yb[par], yq[:, b, :]).then_inc(yb_made, 1)
                pool.wait_ge(cb_in[par], 16 * turn(b, 2))
                pool.nop(nofuse=True)
                for n in range(2):
                    hs = slice(n * XH // 2, (n + 1) * XH // 2)
                    nc.gpsimd.tensor_tensor(cm[par][:, hs, :], cb[par].unsqueeze(1).broadcast_to([P, XH // 2, D]),
                                            headmask[:, hs].unsqueeze(2).broadcast_to([P, XH // 2, D]), ALU.mult).then_inc(cm_made, 1)
            body(0, 0)
            body(1, 1)
            with pool.Fori(1, B // 2) as i:
                body(i * 2, 0)
                body(i * 2 + 1, 1)

        @block.tensor
        def _(pe):
            def scores(b, par, un):
                j, q = un // 2, un % 2
                need(pe, exp_made, NU * b + un - 1)
                nc.tensor.matmul(bank(un % 2), yb[par][:, q * P:(q + 1) * P],
                                 cm[par][:, 2 * j:2 * j + 2, :].rearrange("p o l -> p (o l)"),
                                 start=True, stop=True).then_inc(s_done, 1)

            def ctx_T(b, par):
                pe.wait_ge(cb_in[par], 16 * turn(b, 2))
                need(pe, cT_made, b)
                for l in range(2):
                    last = nc.tensor.transpose(bank(5)[:, l * P:(l + 1) * P], cb[par][:, l * P:(l + 1) * P], ident)
                last.then_inc(cT_done, 1)

            def transposes(b, un):
                pe.wait_ge(exp_made, NU * b + un + 1)
                need(pe, pT_made, NU * b + un - 1)
                for o in range(2):
                    for l in range(2):
                        last = nc.tensor.transpose(bank(2 + un % 2)[:, (2 * o + l) * P:(2 * o + l + 1) * P],
                                                   pr[un % 2][:, o, l * P:(l + 1) * P], ident)
                last.then_inc(pT_done, 1)

            def values(b, par, un):
                j, q = un // 2, un % 2
                pe.wait_ge(pT_made, NU * b + un + 1)
                if un == 0:
                    pe.wait_ge(cT_made, b + 1)
                    need(pe, ret_made, b)
                for o in range(2):
                    for l in range(2):
                        last = nc.tensor.matmul(res_ps[:, q, 2 * j + o, :], prT[un % 2][:, o, l, :], cT[par][:, l, 2 * j + o, :],
                                                start=(l == 0), stop=(l == 1))
                last.then_inc(res_done, 1)

            def result_T(b):
                pe.wait_ge(ret_made, b + 1)
                need(pe, x2_made, b)
                for q in range(2):
                    last = nc.tensor.transpose(rT_ps[:, q * P:(q + 1) * P], ret[:, q].rearrange("p h c -> p (h c)"), ident)
                last.then_inc(rT_done, 1)

            def start(b, par):
                pe.wait_ge(yb_made, b + 1)
                pe.wait_ge(cm_made, 2 * b + 2)

            def body(b, par, last_one):
                for un in range(NU):
                    transposes(b, un)
                    if un + 2 < NU:
                        scores(b, par, un + 2)
                    elif not last_one:
                        if un + 2 == NU:
                            start(b + 1, 1 - par)
                        scores(b + 1, 1 - par, un + 2 - NU)
                    if un:
                        values(b, par, un - 1)
                    elif not (isinstance(b, int) and b == 0):
                        values(b - 1, 1 - par, NU - 1)
                    if un == 1 and not (isinstance(b, int) and b == 0):
                        result_T(b - 1)
                    if un == NU // 2 and not last_one:
                        ctx_T(b + 1, 1 - par)

            ctx_T(0, 0)
            start(0, 0)
            scores(0, 0, 0)
            scores(0, 0, 1)
            sequences(pe, body)
            values(B - 1, 1, NU - 1)
            result_T(B - 1)

        @block.vector
        def _(dve):
            layernorm_stats(nc, dve, None, x1, stats, mv, stat_made, stat_step)
            dve.wait_ge(r_made, 1)
            dve.wait_ge(stat_made, B)
            for b in range(B):
                nc.vector.tensor_scalar(yq[:, b, :], x1[:, b, :], mv[:, b, 0:1], r3[:, b:b + 1],
                                        ALU.subtract, ALU.mult).then_inc(yq_made, 1)
            dve.wait_ge(gam_in, 16)

            def maxima(b, un):
                dve.wait_ge(s_done, NU * b + un + 1)
                need(dve, exp_made, NU * b + un - 1)
                nc.vector.tensor_reduce(nmax[:, un % 2, :], bank(un % 2).rearrange("p (o l) -> p o l", o=2), AX_X, ALU.max,
                                        negate=True).then_inc(max_made, 1)

            def copy_T(b, un):
                dve.wait_ge(pT_done, NU * b + un + 1)
                need(dve, res_done, NU * b + un - 1)
                nc.vector.tensor_copy(prT[un % 2].rearrange("p o l q -> p (o l q)"), bank(2 + un % 2)).then_inc(pT_made, 1)

            def copy_ctx(b, par):
                dve.wait_ge(cT_done, b + 1)
                if not (isinstance(b, int) and b < 2):
                    dve.wait_ge(res_done, NU * b - NU)
                dve.wait_ge(ones_made, 2)
                nc.vector.tensor_copy(cT[par][:, :, :, 0:XD], cT_ps).then_inc(cT_made, 1)

            def divide(b):
                dve.wait_ge(res_done, NU * b + NU)
                need(dve, rT_done, b)
                nc.vector.reciprocal(rec, res_ps[:, :, :, XD:XD + 1]).then_inc(rec_made, 1)
                dve.wait_ge(rec_made, b + 1)
                nc.vector.tensor_tensor(ret, res_ps[:, :, :, 0:XD], rec.broadcast_to([P, 2, XH, XD]), ALU.mult).then_inc(ret_made, 1)

            def add(b):
                dve.wait_ge(rT_done, b + 1)
                nc.vector.scalar_tensor_tensor(x1[:, b, :], rT_ps, gam, x1[:, b, :], ALU.mult, ALU.add).then_inc(x2_made, 1)

            def body(b, par, last_one):
                started = not (isinstance(b, int) and b == 0)
                for un in range(NU):
                    copy_T(b, un)
                    if un + 2 < NU:
                        maxima(b, un + 2)
                    elif not last_one:
                        maxima(b + 1, un + 2 - NU)
                    if un == 0 and started:
                        divide(b - 1)
                    if un == 2 and started:
                        add(b - 1)
                    if un == NU // 2 and not last_one:
                        copy_ctx(b + 1, 1 - par)

            copy_ctx(0, 0)
            maxima(0, 0)
            maxima(0, 1)
            sequences(dve, body)
            divide(B - 1)
            add(B - 1)

        @block.scalar
        def _(act):
            def body(b, par):
                for un in range(NU):
                    act.wait_ge(max_made, NU * b + un + 1)
                    need(act, pT_done, NU * b + un - 1)
                    for o in range(2):
                        last = nc.scalar.activation(pr[un % 2][:, o, :], bank(un % 2)[:, o * D:(o + 1) * D], ACT.Exp,
                                                    bias=nmax[:, un % 2, o:o + 1])
                    last.then_inc(exp_made, 1)
            body(0, 0)
            body(1, 1)
            with act.Fori(1, B // 2) as i:
                body(i * 2, 0)
                body(i * 2 + 1, 1)


def build_route(nc, a, fixed, room, ps, scratch):
    consts, x2, mhalf = fixed["consts"], fixed["x1"], fixed["mhalf"]

    def const(name):
        return consts[:, CONST[name][0]:CONST[name][1]]

    ident = const("ident")
    xf = room.take(B, D)
    xfT = fixed["xfT"]
    wr = room.take(D)
    wrT = room.take(KD, E)
    stats, mv = room.take(B, 6), room.take(B, 2)
    r1, r2 = room.take(B), room.take(B)
    lg = room.take(B, E)
    top = room.take(B, 8)
    idx = room.take(B, 8).bitcast(U32)
    idf = room.take(B, K4)
    ex = room.take(B, K4)
    sm = room.take(B, 1)
    oh = [room.take(B, E) for _ in range(K4)]
    m2 = [room.take(B, E) for _ in range(2)]
    mb = room.take(B, E // 2).bitcast(BF16)
    onesb = room.take(P // 2).bitcast(BF16)
    beforeb = room.take(P // 2).bitcast(BF16)
    tmp = [room.take(B, E) for _ in range(2)]
    pos = room.take(K4, B)
    val, sl, sf = room.take(K4, B), room.take(K4, B), room.take(K4, B)
    wtok, slots = fixed["wtok"], fixed["slots"]
    wsg = room.take(KD, I2)
    wsu = room.take(KD, I2)
    wsd = room.take(2, D)
    ssg = room.take(TOK)
    smT = room.take(2, TOK)
    base = fixed["acc"][1]

    with ExitStack() as ctx:
        def sem(name):
            return ctx.enter_context(nc.semaphore(name))

        wr_in, stat_step, stat_made, r_step, xf_made = sem("wr_in"), sem("rstat_step"), sem("rstat_made"), sem("rr_step"), sem("xf_made")
        wrT_done, wrT_made, xfT_done, xfT_made, lg_done = sem("wrT_done"), sem("wrT_made"), sem("xfT_done"), sem("xfT_made"), sem("lg_done")
        step, ex_in, ex_made, m_made, pos_done, slots_made = sem("route_step"), sem("ex_in"), sem("rexp_made"), sem("choice_made"), sem("pos_done"), sem("slots_made")
        rows_out, cvt, ws_in = sem("rows_out"), sem("bf16_made"), sem("ws_in")
        sh_gate_done, sh_up_done, sh_sg_made, sh_m_made, sh_done, base_made = (
            sem("sh_gate_done"), sem("sh_up_done"), sem("sh_sg_made"), sem("sh_m_made"), sem("sh_done"), sem("base_made"))
        block = ctx.enter_context(nc.Block())
        hps = ps[:, 0:2 * TOK].rearrange("p (k n) -> p k n", k=KD)
        wps = ps[:, 4 * HALF:4 * HALF + KD * E].rearrange("p (k e) -> p k e", k=KD)
        lps = ps[:, 5 * HALF:6 * HALF].rearrange("p (b e) -> p b e", b=B)
        pps = ps[:, 6 * HALF:7 * HALF].rearrange("p (b e) -> p b e", b=B)

        @block.sync
        def _(sp):
            sp.dma_start(wr[0:E], a["w_router"]).then_inc(wr_in, 16)
            for dst, name in ((wsg, "sh_gate"), (wsu, "sh_up")):
                sp.dma_start(dst, a[name].rearrange("(k p) n -> p k n", p=P)).then_inc(ws_in, 16)
            sp.dma_start(wsd[0:IH], a["sh_down"].rearrange("(c p) n -> p c n", p=IH)).then_inc(ws_in, 16)

        @block.tensor
        def _(pe):
            pe.wait_ge(wr_in, 16)
            for k in range(KD):
                last = nc.tensor.transpose(wps[:, k, :], wr[0:E, k * P:(k + 1) * P], ident[0:E, 0:E])
            last.then_inc(wrT_done, 1)
            for b in range(B):
                pe.wait_ge(xf_made, b + 1)
                for k in range(KD):
                    last = nc.tensor.transpose(hps[:, k, b * P:(b + 1) * P], xf[:, b, k * P:(k + 1) * P], ident)
            last.then_inc(xfT_done, 1)
            pe.wait_ge(wrT_made, 1)
            pe.wait_ge(xfT_made, KD)
            for b in range(B):
                for k in range(KD):
                    last = nc.tensor.matmul(lps[:, b, :], xfT[:, k, b * P:(b + 1) * P], wrT[:, k, :],
                                            start=(k == 0), stop=(k == KD - 1))
            last.then_inc(lg_done, 1)

            def shared(c):
                for w, dst, done in ((wsg, ps[:, 0:TOK], sh_gate_done), (wsu, ps[:, TOK:2 * TOK], sh_up_done)):
                    for n in range(2):
                        for k in range(KD):
                            last = nc.tensor.matmul(dst[0:IH, n * HALF:(n + 1) * HALF], w[:, k, c * IH:(c + 1) * IH],
                                                    xfT[:, k, n * HALF:(n + 1) * HALF], start=(k == 0), stop=(k == KD - 1))
                    last.then_inc(done, 1)

            pe.wait_ge(ws_in, 48)
            shared(0)
            pe.wait_ge(m_made, 1)
            pe.wait_ge(cvt, 2)
            for b in range(B):
                for b2 in range(b + 1):
                    last = nc.tensor.matmul(pps[:, b, :], beforeb if b2 == b else onesb, mb[:, b2, :],
                                            start=(b2 == 0), stop=(b2 == b))
            last.then_inc(pos_done, 1)
            pe.wait_ge(sh_m_made, 1)
            shared(1)
            pe.wait_ge(sh_m_made, 2)
            for b in range(B):
                for c in range(2):
                    last = nc.tensor.matmul(ps[:, 2 * TOK + b * D:2 * TOK + (b + 1) * D], smT[0:IH, c, b * P:(b + 1) * P],
                                            wsd[0:IH, c, :], start=(c == 0), stop=(c == 1))
            last.then_inc(sh_done, 1)

        @block.scalar
        def _(act):
            nc.scalar.activation(onesb, const("ones"), ACT.Copy).then_inc(cvt, 1)
            nc.scalar.activation(beforeb, const("before"), ACT.Copy).then_inc(cvt, 1)
            act.wait_ge(wrT_done, 1)
            nc.scalar.activation(wrT, wps, ACT.Copy).then_inc(wrT_made, 1)
            act.wait_ge(xfT_done, 1)
            for k in range(KD):
                nc.scalar.activation(xfT[:, k, :], hps[:, k, :], ACT.Copy).then_inc(xfT_made, 1)
            act.wait_ge(ex_in, 1)
            nc.scalar.activation(ex, ex, ACT.Exp).then_inc(ex_made, 1)
            for c in range(2):
                act.wait_ge(sh_gate_done, c + 1)
                if c:
                    act.wait_ge(sh_m_made, 1)
                nc.scalar.activation(ssg[0:IH], ps[0:IH, 0:TOK], ACT.Silu).then_inc(sh_sg_made, 1)

        @block.vector
        def _(dve):
            n = [0]

            def then(ins):
                n[0] += 1
                ins.then_inc(step, 1)
                dve.wait_ge(step, n[0])

            layernorm_stats(nc, dve, None, x2, stats, mv, stat_made, stat_step)
            dve.wait_ge(r_step, 2)
            for b in range(B):
                nc.vector.tensor_scalar(xf[:, b, :], x2[:, b, :], mv[:, b, 0:1], r2[:, b:b + 1],
                                        ALU.subtract, ALU.mult).then_inc(xf_made, 1)
            dve.wait_ge(lg_done, 1)
            then(nc.vector.tensor_copy(lg, lps))
            for b in range(B):
                last = nc.vector.max(top[:, b, :], lg[:, b, :])
            then(last)
            for b in range(B):
                last = nc.vector.max_index(idx[:, b, :], top[:, b, :], lg[:, b, :])
            then(last)
            nc.vector.tensor_tensor(ex, top[:, :, 0:K4], top[:, :, 0:1].broadcast_to([P, B, K4]), ALU.subtract).then_inc(ex_in, 1)
            then(nc.vector.tensor_copy(idf, idx[:, :, 0:K4]))
            for j in range(K4):
                last = nc.vector.tensor_tensor(oh[j], const("iota").unsqueeze(1).broadcast_to([P, B, E]),
                                               idf[:, :, j:j + 1].broadcast_to([P, B, E]), ALU.is_equal)
            then(last)
            nc.vector.tensor_tensor(m2[0], oh[0], oh[1], ALU.add)
            then(nc.vector.tensor_tensor(m2[1], oh[2], oh[3], ALU.add))
            nc.vector.tensor_tensor(mb, m2[0], m2[1], ALU.add).then_inc(m_made, 1)
            dve.wait_ge(ex_made, 1)
            then(nc.vector.tensor_reduce(sm.rearrange("p b o -> p (b o)"), ex, AX_X, ALU.add))
            then(nc.vector.reciprocal(sm, sm))
            nc.vector.tensor_tensor(wtok, ex, sm.broadcast_to([P, B, K4]), ALU.mult)
            dve.wait_ge(pos_done, 1)
            for j in range(K4):
                then(nc.vector.tensor_tensor(tmp[j % 2], oh[j], pps, ALU.mult))
                then(nc.vector.tensor_reduce(pos[:, j, :], tmp[j % 2], AX_X, ALU.add))
            nc.vector.tensor_scalar(val, pos, float(C), None, ALU.is_lt)
            then(nc.vector.scalar_tensor_tensor(sl, idf.rearrange("p b j -> p j b"), float(C), pos, ALU.mult, ALU.add))
            then(nc.vector.scalar_tensor_tensor(sf, sl, float(-SLOTS), val, ALU.add, ALU.mult))
            nc.vector.tensor_scalar(slots, sf, float(SLOTS), None, ALU.add).then_inc(slots_made, 1)
            for c in range(2):
                dve.wait_ge(sh_sg_made, c + 1)
                dve.wait_ge(sh_up_done, c + 1)
                nc.vector.tensor_tensor(smT[0:IH, c, :], ssg[0:IH], ps[0:IH, TOK:2 * TOK], ALU.mult).then_inc(sh_m_made, 1)
            dve.wait_ge(sh_done, 1)
            nc.vector.tensor_tensor(base.rearrange("p b d -> p (b d)"), x2.rearrange("p b d -> p (b d)"),
                                    ps[:, 2 * TOK:4 * TOK], ALU.add).then_inc(base_made, 1)

        @block.gpsimd
        def _(pool):
            pool.wait_ge(stat_made, B)
            nc.gpsimd.tensor_scalar(r1, mv[:, :, 1], 1e-5, None, ALU.add).then_inc(r_step, 1)
            pool.wait_ge(r_step, 1)
            nc.gpsimd.tensor_tensor(r2, r1, mhalf.broadcast_to([P, B]), ALU.pow).then_inc(r_step, 1)
            pool.wait_ge(slots_made, 1)
            for b in range(B):
                for j in range(K4):
                    nc.gpsimd.indirect_dma_start(
                        scratch["rows"], bass.IndirectOffsetOnAxis(slots[:, j, b:b + 1], 0), xf[:, b, :], None,
                        bounds_check=SLOTS - 1, oob_is_err=False).then_inc(rows_out, 16)
            pool.wait_ge(rows_out, 16 * B * K4)


def build_experts(nc, a, fixed, room, ps, scratch, ring, ring_in, out):
    consts, x2, xfT, wtok, slots = fixed["consts"], fixed["x1"], fixed["xfT"], fixed["wtok"], fixed["slots"]
    ident = consts[:, CONST["ident"][0]:CONST["ident"][1]]
    xg = [room.take(D) for _ in range(RING)]
    xT = [room.take(KD, P) for _ in range(2)]
    sg = [room.take(I2) for _ in range(2)]
    gu = [room.take(I2) for _ in range(2)]
    guT = [room.take(2, P) for _ in range(2)]
    y = [room.take(D) for _ in range(2)]
    yg = [room.take(K4, D) for _ in range(4)]
    acc = fixed["acc"]

    def bank(i):
        return ps[:, i * HALF:(i + 1) * HALF]

    with ExitStack() as ctx:
        def sem(name):
            return ctx.enter_context(nc.semaphore(name))

        xg_in = [sem(f"xg_in{i}") for i in range(RING)]
        xT_done, xT_made, gu_done, sg_made, gu_made = sem("xT_done"), sem("xT_made"), sem("gu_done"), sem("esg_made"), sem("gu_made")
        guT_done, guT_made, y_done, y_made = sem("guT_done"), sem("guT_made"), sem("y_done"), sem("y_made")
        y_out = [sem(f"y_out{i}") for i in range(2)]
        yg_in = [sem(f"yg_in{i}") for i in range(4)]
        acc_step, out_done = sem("acc_step"), sem("out_done")
        block = ctx.enter_context(nc.Block())

        def groups(eng, body):
            body(-1, RING - 1, False, True)
            for s in range(RING):
                body(s, s, True, True)
            with eng.Fori(1, (NG - RING) // RING) as i:
                for s in range(RING):
                    body(i * RING + s, s, True, True)
            for s in range(RING):
                body(NG - RING + s, s, True, s < RING - 1)

        @block.sync
        def _(sp):
            def rows(g, slot):
                sp.dma_start(xg[slot], scratch["rows"].rearrange("(g p) d -> g p d", p=P)[g]).then_inc(xg_in[slot], 16)
            for g in range(RING):
                rows(g, g)
            with sp.Fori(0, (NG - RING) // RING) as i:
                for s in range(RING):
                    sp.wait_ge(xT_done, i * RING + (s + 1))
                    sp.nop(nofuse=True)
                    rows(i * RING + (s + RING), s)
                    sp.wait_ge(gu_done, i * RING + (s + 1))
                    sp.nop(nofuse=True)
                    gate_up_loads(sp, a, ring, i * RING + (s + RING), s, ring_in[s])
                    sp.wait_ge(y_done, i * RING + (s + 1))
                    sp.nop(nofuse=True)
                    down_load(sp, a, ring, i * RING + (s + RING), s, ring_in[s])

        @block.tensor
        def _(pe):
            def body(g, s, back, front):
                f, fs = g + 1, (s + 1) % RING
                par, fpar = s % 2, (s + 1) % 2
                if front:
                    pe.wait_ge(xg_in[fs], 16 * turn(f, RING))
                    need(pe, xT_made, f - 1)
                    for k in range(KD):
                        last = nc.tensor.transpose(bank(fpar)[:, k * P:(k + 1) * P],
                                                   xg[fs].rearrange("p (c k) -> p k c", k=KD)[:, k, :], ident)
                    last.then_inc(xT_done, 1)
                if back:
                    pe.wait_ge(gu_made, g + 1)
                    for c in range(2):
                        last = nc.tensor.transpose(bank(4 + par)[0:IH, c * P:(c + 1) * P],
                                                   gu[par].rearrange("p (i c) -> p c i", c=2)[:, c, :], ident)
                    last.then_inc(guT_done, 1)
                if front:
                    pe.wait_ge(xT_made, f + 1)
                    pe.wait_ge(ring_in[fs], LOADS * turn(f, RING))
                    need(pe, gu_made, f - 1)
                    for e in range(GRP):
                        for k in range(KD):
                            last = nc.tensor.matmul(bank(2 + fpar)[e * C:(e + 1) * C, 0:2 * I2], xT[fpar][:, k, e * C:(e + 1) * C],
                                                    ring["wgu"][fs][:, e, k, :], start=(k == 0), stop=(k == KD - 1))
                    last.then_inc(gu_done, 1)
                if back:
                    pe.wait_ge(guT_made, g + 1)
                    need(pe, y_made, g)
                    for e in range(GRP):
                        for c in range(2):
                            last = nc.tensor.matmul(bank(6 + par)[e * C:(e + 1) * C, 0:D], guT[par][0:IH, c, e * C:(e + 1) * C],
                                                    ring["wd"][s][0:IH, e, c, :], start=(c == 0), stop=(c == 1))
                    last.then_inc(y_done, 1)

            groups(pe, body)

        @block.scalar
        def _(act):
            def body(g, s, back, front):
                f = g + 1
                par, fpar = s % 2, (s + 1) % 2
                if front:
                    act.wait_ge(gu_done, f + 1)
                    need(act, gu_made, f - 1)
                    nc.scalar.activation(sg[fpar], bank(2 + fpar)[:, 0:I2], ACT.Silu).then_inc(sg_made, 1)
                if back:
                    act.wait_ge(y_done, g + 1)
                    if not (isinstance(g, int) and g < 2):
                        act.wait_ge(y_out[par], 16 * turn(g, 2) - 16)
                    nc.scalar.activation(y[par], bank(6 + par)[:, 0:D], ACT.Copy).then_inc(y_made, 1)
                    act.wait_ge(y_made, g + 1)
                    act.dma_start(scratch["results"][0:SLOTS].rearrange("(g p) d -> g p d", p=P)[g], y[par]).then_inc(y_out[par], 16)

            groups(act, body)
            for b in range(B):
                act.wait_ge(acc_step, K4 * (b + 1))
                act.dma_start(out[b], acc[(K4 - 1) % 2][:, b, :]).then_inc(out_done, 16)
            act.wait_ge(out_done, 16 * B)

        @block.vector
        def _(dve):
            def body(g, s, back, front):
                f = g + 1
                par, fpar = s % 2, (s + 1) % 2
                if front:
                    dve.wait_ge(xT_done, f + 1)
                    need(dve, gu_done, f - 1)
                    nc.vector.tensor_copy(xT[fpar].rearrange("p k c -> p (k c)"), bank(fpar)[:, 0:D]).then_inc(xT_made, 1)
                if back:
                    dve.wait_ge(guT_done, g + 1)
                    nc.vector.tensor_copy(guT[par][0:IH].rearrange("p c n -> p (c n)"), bank(4 + par)[0:IH, 0:2 * P]).then_inc(guT_made, 1)
                if front:
                    dve.wait_ge(sg_made, f + 1)
                    need(dve, guT_done, f - 1)
                    nc.vector.tensor_tensor(gu[fpar], sg[fpar], bank(2 + fpar)[:, I2:2 * I2], ALU.mult).then_inc(gu_made, 1)

            groups(dve, body)
            for b in range(B):
                dve.wait_ge(yg_in[b % 4], 16 * K4 * (b // 4 + 1))
                for j in range(K4):
                    if j:
                        dve.wait_ge(acc_step, K4 * b + j)
                    nc.vector.scalar_tensor_tensor(acc[j % 2][:, b, :],
                                                   yg[b % 4][:, j, :], wtok[:, b, j:j + 1], acc[(j + 1) % 2][:, b, :],
                                                   ALU.mult, ALU.add).then_inc(acc_step, 1)

        @block.gpsimd
        def _(pool):
            for par in range(2):
                pool.wait_ge(y_out[par], 16 * (NG // 2))
            for b in range(B):
                if b >= 4:
                    pool.wait_ge(acc_step, K4 * (b - 3))
                for j in range(K4):
                    nc.gpsimd.indirect_dma_start(yg[b % 4][:, j, :], None, scratch["results"],
                                                 bass.IndirectOffsetOnAxis(slots[:, j, b:b + 1], 0),
                                                 bounds_check=SLOTS, oob_is_err=True).then_inc(yg_in[b % 4], 16)


def turn(g, n):
    return g // n + 1


NAMES = {
    "x": "x", "ctx": "ctx_2048", "wq": "L0_attn_wq", "wk": "L0_attn_wk", "wv": "L0_attn_wv", "conv_q": "L0_attn_conv_q",
    "conv_k": "L0_attn_conv_k", "conv_v": "L0_attn_conv_v", "wfa": "L0_attn_wfa", "wfb": "L0_attn_wfb", "wb": "L0_attn_wb",
    "wga": "L0_attn_wga", "wgb": "L0_attn_wgb", "a_log": "L0_attn_a_log", "dt_bias": "L0_attn_dt_bias",
    "o_norm_w": "L0_attn_o_norm_w", "wo": "L0_attn_wo", "ln1_w": "L0_attn_ln1_w", "ln2_w": "L0_attn_ln2_w",
    "w_gate": "L0_attn_w_gate", "w_up": "L0_attn_w_up", "w_down": "L0_attn_w_down", "gamma": "L0_xattn_gamma",
    "w_router": "L0_ffn_w_router", "e_gate": "L0_ffn_w_gate", "e_up": "L0_ffn_w_up", "e_down": "L0_ffn_w_down",
    "sh_gate": "L0_ffn_w_sh_gate", "sh_up": "L0_ffn_w_sh_up", "sh_down": "L0_ffn_w_sh_down",
}
ARENA = 53200


def decoder_kernel(nc, a, out, scratch):
    with ExitStack() as ctx:
        arena = ctx.enter_context(nc.sbuf_tensor("arena", [P, ARENA], F32))
        psum = ctx.enter_context(nc.psum_tensor("psum", [P, 8 * HALF], F32))
        wo_in = ctx.enter_context(nc.semaphore("wo_in"))
        ring_in = [ctx.enter_context(nc.semaphore(f"ring_in{i}")) for i in range(RING)]
        ps = psum[:, :]
        base = Room(arena, 0)
        fixed = {"consts": base.take(NCONST), "mhalf": base.take(1), "onw": base.take(1), "x0": base.take(B, D)}
        low = base.at
        fixed["hT"] = base.take(KD, TOK)
        fixed["lowg"] = base.take(TOK)
        fixed["heads"] = base.take(H, HT)
        after_prepare = base.at
        prep = Room(arena, after_prepare)
        clear_semaphores(nc, build_prepare(nc, a, fixed, prep, ps))
        fixed["o_all"] = base.take(H, TOK)
        split = (KD + 1) * TOK // D
        wo = [Room(arena, low).take(split, D), Room(arena, ARENA - (H - split) * D).take(H - split, D)]
        clear_semaphores(nc, build_delta(nc, a, fixed, base, ps, wo, wo_in))
        assert base.at <= ARENA - (H - split) * D

        fixed["x1"] = Room(arena, low).take(B, D)
        build_mlp(nc, a, fixed, Room(arena, after_prepare + H * TOK), ps, wo, wo_in)

        rest = Room(arena, low + B * D)
        ring = {"wgu": [rest.take(GRP, KD, 2 * I2) for _ in range(RING)], "wd": [rest.take(GRP, 2, D) for _ in range(RING)]}
        fixed["xfT"] = rest.take(KD, TOK)
        fixed["wtok"] = rest.take(B, K4)
        fixed["acc"] = [rest.take(B, D) for _ in range(2)]
        fixed["slots"] = rest.take(K4, B).bitcast(U32)
        build_cross(nc, a, fixed, Room(arena, rest.at), ps, ring, ring_in, scratch)
        build_route(nc, a, fixed, Room(arena, rest.at), ps, scratch)
        build_experts(nc, a, fixed, Room(arena, rest.at), ps, scratch, ring, ring_in, out)


def kernel(**inputs):
    import numpy as np
    import concourse.bacc as bacc
    from concourse.bass_utils import run_bass_kernel_spmd

    nc = bacc.Bacc("TRN2", target_bir_lowering=False, num_devices=1)
    arrays, a = {}, {}
    for name, full in NAMES.items():
        v = np.ascontiguousarray(inputs[full])
        if v.ndim == 0:
            v = v.reshape(1)
        arrays["in_" + name] = v
    arrays["in_consts"] = constant_table(np)
    for key, v in arrays.items():
        a[key[3:]] = nc.dram_tensor(key, v.shape, mybir.dt.from_np(v.dtype), kind="ExternalInput").ap()
    out = nc.dram_tensor("out", (B, P, D), F32, kind="ExternalOutput").ap()
    scratch = {"rows": nc.dram_tensor("rows", (SLOTS, D), F32, kind="Internal").ap(),
               "results": nc.dram_tensor("results", (SLOTS + 1, D), F32, kind="Internal").ap()}
    decoder_kernel(nc, a, out, scratch)
    got = run_bass_kernel_spmd(nc, [arrays], core_ids=[0])
    return got.results[0]["out"]
```
